# Optimizing a Trainium2 kernel written in Bass

```python
import numpy as np
import jax
import jax.numpy as jnp

def _softmax(x, axis=-1):
    return jax.nn.softmax(x, axis=axis)

def _gelu(x):
    return jax.nn.gelu(x, approximate=True)

def _silu(x):
    return jax.nn.silu(x)

def _sigmoid(x):
    return jax.nn.sigmoid(x)

def _layernorm(x, axis=-1, eps=1e-05):
    m = jnp.mean(x, axis=axis, keepdims=True)
    v = jnp.var(x, axis=axis, keepdims=True)
    return (x - m) / jnp.sqrt(v + eps)

def _scatter_add(tgt, idx, src, axis=0):
    return tgt.at[idx].add(src)

def _segment_sum(src, seg, n):
    return jax.ops.segment_sum(src, seg, n)
kernel_name = 'mk_gnn_resnorm_d1_gnn_r64_133a4c'

def setup_inputs(seed: int=0):
    np.random.seed(seed)
    _w = jnp.asarray

    def _rec_inputs():
        import jax
        import jax.numpy as jnp
        _gk = jax.random.key(seed)
        x = -0.0002117 + 1 * jax.random.normal(jax.random.fold_in(_gk, 1), (50000, 256), jnp.float32)
        src = jax.random.randint(jax.random.fold_in(_gk, 2), (12500,), 0, 50000, jnp.int32)
        dst = jnp.minimum((50000 * jax.random.uniform(jax.random.fold_in(_gk, 3), (12500,)) ** 2.0).astype(jnp.int32), 49999)
        _o = jnp.argsort(dst, stable=True)
        src = src[_o]
        dst = dst[_o]
        edge_attr_256 = -6.47781e-05 + 0.999943 * jax.random.normal(jax.random.fold_in(_gk, 11), (12500, 256), jnp.float32)
        return (x, src, dst, edge_attr_256)
    x, src, dst, edge_attr_256 = _rec_inputs()

    def _L0_gnn_setup():
        import jax, jax.numpy as jnp
        import numpy as np
        N_VERTEX = 100000
        N_EDGE = 12500
        HIDDEN = 256
        key = jax.random.key(seed)
        ks = jax.random.split(key, 10)
        d = HIDDEN
        vertex_features = jax.random.normal(ks[0], (N_VERTEX, d), dtype=jnp.float32)
        edge_features = jax.random.normal(ks[1], (N_EDGE, d), dtype=jnp.float32)
        edge_index = jax.random.randint(ks[2], (2, N_EDGE), 0, N_VERTEX, dtype=jnp.int64)

        def lin(k, fan_in, fan_out):
            lim = 1.0 / np.sqrt(fan_in)
            kw, kb = jax.random.split(k)
            W = jax.random.uniform(kw, (fan_in, fan_out), minval=-lim, maxval=lim, dtype=jnp.float32)
            b = jax.random.uniform(kb, (fan_out,), minval=-lim, maxval=lim, dtype=jnp.float32)
            return (W, b)
        W1, b1 = lin(ks[3], 2 * d, d)
        W2, b2 = lin(ks[4], d, d)
        W3, b3 = lin(ks[5], d, d)
        return {'vertex_features': vertex_features, 'edge_features': edge_features, 'edge_index': edge_index, 'W1': W1, 'b1': b1, 'W2': W2, 'b2': b2, 'W3': W3, 'b3': b3}
    _L0_gnn_all = _L0_gnn_setup()
    _L0_gnn_in = {k: v for k, v in _L0_gnn_all.items() if k in ('W1', 'b1', 'W2', 'b2', 'W3', 'b3')}
    del _L0_gnn_all
    return {'x': x, 'src': src, 'dst': dst, 'edge_attr_256': edge_attr_256, 'L0_gnn_W1': _L0_gnn_in['W1'], 'L0_gnn_b1': _L0_gnn_in['b1'], 'L0_gnn_W2': _L0_gnn_in['W2'], 'L0_gnn_b2': _L0_gnn_in['b2'], 'L0_gnn_W3': _L0_gnn_in['W3'], 'L0_gnn_b3': _L0_gnn_in['b3']}

def reference(x, src, dst, edge_attr_256, L0_gnn_W1, L0_gnn_b1, L0_gnn_W2, L0_gnn_b2, L0_gnn_W3, L0_gnn_b3):
    import jax
    import jax.numpy as jnp

    def _L0_gnn_ref(vertex_features, edge_features, edge_index, W1, b1, W2, b2, W3, b3):
        import jax, jax.numpy as jnp
        import numpy as np
        N_VERTEX = 100000
        N_EDGE = 12500
        HIDDEN = 256
        num_vertex = vertex_features.shape[0]
        receivers_idx = edge_index[1]
        aggr = jax.ops.segment_sum(edge_features, receivers_idx, num_segments=num_vertex)
        collected = jnp.concatenate([vertex_features, aggr], axis=-1)
        h = jax.nn.relu(collected @ W1 + b1)
        h = jax.nn.relu(h @ W2 + b2)
        return h @ W3 + b3
    edge_index = jnp.stack([src, dst])
    x = _layernorm(x + _L0_gnn_ref(x, edge_attr_256, edge_index, L0_gnn_W1, L0_gnn_b1, L0_gnn_W2, L0_gnn_b2, L0_gnn_W3, L0_gnn_b3), axis=-1)
    return x

_drawn_inputs = setup_inputs


def setup_inputs(seed=0):
    import zlib

    import numpy as np

    out = dict(_drawn_inputs(seed))
    spreads = {}
    factors = {'L0_gnn_b1': 8.0, 'L0_gnn_b2': 3.928}
    for name, (base, spread) in spreads.items():
        noise = np.random.default_rng([zlib.crc32(name.encode()), seed]).standard_normal(out[name].shape)
        drawn = base * np.exp(spread * noise) if base else spread * noise
        out[name] = jnp.asarray(drawn.astype(out[name].dtype))
    for name, factor in factors.items():
        out[name] = (out[name] * factor).astype(out[name].dtype)
    return out
```

```python
import concourse.bass as bass
from concourse import mybir
from contextlib import ExitStack

FP32 = mybir.dt.float32
FP32R = mybir.dt.float32r
BF16 = mybir.dt.bfloat16
INT32 = mybir.dt.int32
ALU = mybir.AluOpType
ACT = mybir.ActivationFunctionType

LANES = 128
SUB = 4
STEP = LANES * SUB
RING = 4
EPS = 1e-5


class Step:

    def __init__(self, i, c):
        self.i, self.c = i, c

    def __add__(self, o):
        return Step(self.i, self.c + o)

    def __sub__(self, o):
        return Step(self.i, self.c - o)

    def count(self, per=1, plus=0):
        return self.i * (RING * per) + (self.c * per + plus)

    def turns(self, ring, per=1, plus=0):
        return self.i * (RING // ring * per) + (self.c // ring * per + plus)

    def slot(self, ring):
        return self.c % ring


def reached(engine, semaphore, value):
    if isinstance(value, int) and value <= 0:
        return
    engine.wait_ge(semaphore, value)


def bass_gnn_residual_norm(nc, x, src, dst, edges, w1, b1, w2, b2, w3, b3, out):
    nodes, D = x.shape
    n_edges = edges.shape[0]
    KD = D // LANES

    tiles = nodes // (2 * STEP)
    assert tiles % 2 == 0
    PLAIN = 2 * tiles
    tail_rows = nodes - PLAIN * STEP
    tail_lanes = tail_rows // (2 * SUB)
    assert tail_rows == tail_lanes * 2 * SUB and 0 < tail_lanes <= LANES
    FIRST_EDGE = PLAIN + 2
    GROUPS = n_edges // STEP
    assert GROUPS % RING == 0 and GROUPS >= RING
    edge_tail = n_edges - GROUPS * STEP
    TAIL_SUB = 2
    edge_lanes = edge_tail // TAIL_SUB
    assert edge_tail == edge_lanes * TAIL_SUB and 0 < edge_lanes <= LANES
    CHUNKS = GROUPS * SUB + TAIL_SUB
    STEPS = FIRST_EDGE + GROUPS + 1

    CLEAR = 3 * STEP
    CLEARS = -(-(nodes + LANES) // CLEAR)
    ADD0 = -(-(max(CLEARS, GROUPS) + 2) // RING) * RING
    ADD_END = ADD0 + 2 * GROUPS
    PAIRS = 2 * GROUPS + 1
    assert ADD_END + RING <= PLAIN

    def lanes(c):
        return tail_lanes if PLAIN <= c < FIRST_EDGE else edge_lanes if c == STEPS - 1 else LANES

    def subs(c):
        return TAIL_SUB if c == STEPS - 1 else SUB

    def exists(step):
        return 0 <= step.c < STEPS

    def is_edge_step(step):
        return FIRST_EDGE <= step.c < STEPS

    def is_tail(step):
        return step.c == PLAIN or step.c == PLAIN + 1

    loops = [(2 * RING, min(GROUPS, CLEARS) - RING), (ADD0 + RING, ADD_END - RING),
             (ADD_END + RING, PLAIN - RING), (FIRST_EDGE + 6, FIRST_EDGE + GROUPS - 3)]

    def run_slots(engine, slot):
        at = 0
        for begin, end in loops:
            turns = (end - begin) // RING
            if turns < 1:
                continue
            for c in range(at, begin):
                slot(Step(0, c))
            with engine.Fori(0, turns) as i:
                for k in range(RING):
                    slot(Step(i, begin + k))
            at = begin + turns * RING
        for c in range(at, STEPS + 3):
            slot(Step(0, c))

    table = nc.dram_tensor("aggr_table", (CLEARS * CLEAR, D), FP32).ap()

    ctx = ExitStack()
    with ctx:
        def sb(name, shape, dt=FP32):
            return ctx.enter_context(nc.sbuf_tensor(name, shape, dt))

        def sem(name):
            return ctx.enter_context(nc.semaphore(name))

        raw = {n: sb(f"raw_{n}", [LANES, KD, D]) for n in ("w1x", "w1a", "w2", "w3")}
        w_hi = {n: sb(f"hi_{n}", [LANES, KD, D], FP32R) for n in raw}
        w_lo = {n: sb(f"lo_{n}", [LANES, KD, D], FP32R) for n in raw}
        bias1 = sb("bias1", [LANES, KD])
        bias2 = sb("bias2", [LANES, KD])
        bias3 = sb("bias3", [LANES, D])
        eps = sb("eps", [LANES, 1])
        zeros = sb("zeros", [LANES, CLEAR // LANES * D])
        identity = sb("identity", [LANES, LANES])
        earlier = sb("earlier", [LANES, LANES])
        lane = sb("lane", [LANES, 1])
        lane_i = sb("lane_i", [LANES, 1], INT32)

        xin = sb("xin", [LANES, 2, 2, SUB, D])
        xb3 = sb("xb3", [LANES, RING, SUB, D])
        y = sb("y", [LANES, 2, 2, SUB, D])
        aggr = sb("aggr", [LANES, 2, SUB, D])
        x_hi = sb("x_hi", [LANES, KD, STEP], FP32R)
        x_lo = sb("x_lo", [LANES, KD, STEP], FP32R)
        a_hi = sb("a_hi", [LANES, KD, STEP], FP32R)
        a_lo = sb("a_lo", [LANES, KD, STEP], FP32R)
        h = sb("h", [LANES, 2, KD, STEP])
        h1_hi = sb("h1_hi", [LANES, 2, KD, STEP], FP32R)
        h1_lo = sb("h1_lo", [LANES, 2, KD, STEP], FP32R)
        h2_hi = sb("h2_hi", [LANES, 2, KD, STEP], FP32R)
        h2_lo = sb("h2_lo", [LANES, 2, KD, STEP], FP32R)
        stats = sb("stats", [LANES, SUB, 6])
        mean_var = sb("mean_var", [LANES, 2, SUB, 2])
        std = sb("std", [LANES, 2, SUB])
        rstd = sb("rstd", [LANES, SUB])
        dst_i = sb("dst_i", [LANES, CHUNKS], INT32)
        dst_f = sb("dst_f", [LANES, CHUNKS])
        own_i = sb("own_i", [LANES, CHUNKS], INT32)
        out_i = sb("out_i", [LANES, CHUNKS], INT32)
        dst_row = sb("dst_row", [LANES, 2, STEP], INT32)
        e_in = sb("e_in", [LANES, 2, SUB, D])
        same = sb("same", [LANES, 2, 2, LANES])
        sums = sb("sums", [LANES, 2, 2, D])
        before = sb("before", [LANES, SUB, LANES], BF16)
        above = sb("above", [LANES, SUB * (SUB - 1) // 2, LANES], BF16)
        n_before = sb("n_before", [LANES, SUB])
        n_above = sb("n_above", [LANES, SUB])
        n_both = sb("n_both", [LANES, SUB])
        to_spare = sb("to_spare", [LANES, SUB])
        shift = sb("shift", [LANES, 2, SUB])
        add_at = sb("add_at", [LANES, 2, SUB], INT32)
        x_from = sb("x_from", [LANES, 2, SUB], INT32)
        aggr_from = sb("aggr_from", [LANES, 2, SUB], INT32)
        out_at = sb("out_at", [LANES, 2, SUB], INT32)

        xT = ctx.enter_context(nc.psum_tensor("xT", [LANES, KD, STEP], FP32))
        z1 = ctx.enter_context(nc.psum_tensor("z1", [LANES, KD, STEP], FP32))
        z2 = ctx.enter_context(nc.psum_tensor("z2", [LANES, KD, STEP], FP32))
        z3 = ctx.enter_context(nc.psum_tensor("z3", [LANES, SUB, D], FP32))

        weights_loaded, biases_loaded = sem("weights_loaded"), sem("biases_loaded")
        dst_loaded = sem("dst_loaded")
        weights_high, weights_split = sem("weights_high"), sem("weights_split")
        constants = sem("constants")
        masks_cleared = sem("masks_cleared")
        spare_known, dst_f_known = sem("spare_known"), sem("dst_f_known")
        x_loaded = [sem(f"x_loaded{n}") for n in range(2)]
        x_gathered = [sem(f"x_gathered{n}") for n in range(RING)]
        aggr_gathered = [sem(f"aggr_gathered{n}") for n in range(2)]
        x_transposed, x_high, x_split = sem("x_transposed"), sem("x_high"), sem("x_split")
        aggr_transposed, aggr_high, aggr_split = (
            sem("aggr_transposed"), sem("aggr_high"), sem("aggr_split"))
        z1_done, h1_relu, h1_high, h1_split = (
            sem("z1_done"), sem("h1_relu"), sem("h1_high"), sem("h1_split"))
        z2_done, h2_relu, h2_high, h2_split = (
            sem("z2_done"), sem("h2_relu"), sem("h2_high"), sem("h2_split"))
        z3_done, xb3_done, y_summed = sem("z3_done"), sem("xb3_done"), sem("y_summed")
        stats_done, mean_var_done = sem("stats_done"), sem("mean_var_done")
        std_done, rstd_done, y_done = sem("std_done"), sem("rstd_done"), sem("y_done")
        stored = [sem(f"stored{n}") for n in range(2)]
        scattered = [sem(f"scattered{n}") for n in range(RING)]
        dst_row_loaded = [sem(f"dst_row_loaded{n}") for n in range(2)]
        e_loaded = [sem(f"e_loaded{n}") for n in range(2)]
        n_before_done, n_both_done, to_spare_done, shift_done, own_known = (
            sem("n_before_done"), sem("n_both_done"), sem("to_spare_done"), sem("shift_done"),
            sem("own_known"))
        cleared = sem("cleared")
        added = sem("added")
        pool_passed, dve_passed = sem("pool_passed"), sem("dve_passed")
        add_at_set, x_from_set, aggr_from_set, out_at_set = (
            sem("add_at_set"), sem("x_from_set"), sem("aggr_from_set"),
            sem("out_at_set"))
        same_done, sums_done, sums_copied = (
            sem("same_done"), sem("sums_done"), sem("sums_copied"))

        block = ctx.enter_context(nc.Block())

        def pair_of(s):
            pair = s - ADD0
            if not 0 <= pair.c < PAIRS:
                return None
            group = pair.turns(2)
            if pair.c == PAIRS - 1:
                return pair, group, edge_lanes, 0, TAIL_SUB
            return pair, group, LANES, 2 * pair.slot(2), SUB

        def marking_group(s):
            if s.c > GROUPS:
                return None
            return (s, edge_lanes, TAIL_SUB) if s.c == GROUPS else (s, LANES, SUB)

        def dst_rows_of(group_c, sub, n_lanes, n_sub):
            v = dst_row[0:n_lanes, group_c % 2, 0:n_lanes * n_sub]
            return v.rearrange("q (p j) -> q j p", j=n_sub)[:, sub]

        @block.sync
        def _(sp):
            def load_tile(step):
                n = step.turns(2)
                if is_tail(step):
                    rows = x[PLAIN * STEP:nodes, :].rearrange("(p j) d -> p (j d)", j=2 * SUB)
                    to = xin[0:tail_lanes, step.c // 2 % 2, :, :, :]
                else:
                    rows = x[bass.ds(n * (2 * STEP), 2 * STEP), :].rearrange(
                        "(p j) d -> p (j d)", j=2 * SUB)
                    to = xin[:, step.c // 2 % 2, :, :, :]
                sp.dma_start(to.rearrange("p t j d -> p (t j d)"), rows).then_inc(
                    x_loaded[step.c // 2 % 2], 16)

            def load_dst_row(group_c, group, n_edges_of):
                sp.dma_start(dst_row[:, group_c % 2, 0:n_edges_of],
                             dst[bass.ds(group * STEP, n_edges_of)].unsqueeze(0).to_broadcast(
                                 [LANES, n_edges_of])).then_inc(dst_row_loaded[group_c % 2], 16)

            def load_edges(group_c, group, n_lanes, n_sub):
                sp.dma_start(e_in[0:n_lanes, group_c % 2, 0:n_sub, :].rearrange("p j d -> p (j d)"),
                             edges[bass.ds(group * STEP, n_lanes * n_sub), :].rearrange(
                                 "(p j) d -> p (j d)", j=n_sub)).then_inc(e_loaded[group_c % 2], 16)

            load_tile(Step(0, 0))
            halves = (("w1x", w1[0:D, :]), ("w1a", w1[D:2 * D, :]), ("w2", w2), ("w3", w3))
            for name, w in halves:
                sp.dma_start(raw[name][:, :, :], w.rearrange("(k p) n -> p k n", p=LANES)).then_inc(
                    weights_loaded, 16)
            with nc.allow_non_contiguous_dma(reason="two biases of 256 words, once"):
                for to, b in ((bias1, b1), (bias2, b2)):
                    sp.dma_start(to[:, :], b.rearrange("(k p) -> p k", p=LANES)).then_inc(
                        biases_loaded, 16)
            sp.dma_start(bias3[:, :], b3.unsqueeze(0).to_broadcast([LANES, D])).then_inc(
                biases_loaded, 16)
            sp.dma_start(dst_i[:, 0:GROUPS * SUB].rearrange("p (g j) -> p g j", j=SUB),
                         dst[0:GROUPS * STEP].rearrange("(g p j) -> p g j", p=LANES, j=SUB)
                         ).then_inc(dst_loaded, 16)
            sp.dma_start(dst_i[0:edge_lanes, GROUPS * SUB:CHUNKS],
                         dst[GROUPS * STEP:n_edges].rearrange("(p j) -> p j", j=TAIL_SUB)
                         ).then_inc(dst_loaded, 16)
            load_dst_row(0, 0, STEP)
            load_tile(Step(0, 2))

            sp.wait_ge(constants, 5)

            def slot(s):
                if s.c < CLEARS:
                    sp.dma_start(table[bass.ds(s.count(CLEAR), CLEAR), :].rearrange(
                        "(p j) d -> p (j d)", p=LANES), zeros[:, :]).then_inc(cleared, 16)
                if s.c % 2 == 1 and s.c + 3 <= PLAIN:
                    reached(sp, x_transposed, s.count(plus=1))
                    reached(sp, xb3_done, s.count(plus=1))
                    load_tile(s + 3)
                g = s + 1
                if g.c <= GROUPS:
                    reached(sp, own_known, g.count(plus=-1))
                    load_dst_row(g.c, g.count(), edge_tail if g.c == GROUPS else STEP)
                ahead = s + 2 - ADD0
                if ahead.c >= 0 and ahead.c % 2 == 0 and ahead.c < PAIRS:
                    gc, group = ahead.c // 2, ahead.turns(2)
                    last = gc == GROUPS
                    reached(sp, sums_done, ahead.count(plus=-2))
                    reached(sp, same_done, ahead.count(plus=-2))
                    if gc < 2:
                        reached(sp, own_known, GROUPS + 1)
                    load_dst_row(gc + GROUPS + 1, group, edge_tail if last else STEP)
                    load_edges(gc, group, edge_lanes if last else LANES, TAIL_SUB if last else SUB)
                done = s - 4
                if done.c >= 0 and done.c % 2 == 0 and done.c <= PLAIN:
                    reached(sp, y_done, done.count(plus=2))
                    if is_tail(done):
                        rows = out[PLAIN * STEP:nodes, :].rearrange("(p j) d -> p (j d)", j=2 * SUB)
                        of = y[0:tail_lanes, done.c // 2 % 2, :, :, :]
                    else:
                        rows = out[bass.ds(done.turns(2) * (2 * STEP), 2 * STEP), :].rearrange(
                            "(p j) d -> p (j d)", j=2 * SUB)
                        of = y[:, done.c // 2 % 2, :, :, :]
                    sp.dma_start(rows, of.rearrange("p t j d -> p (t j d)")).then_inc(
                        stored[done.c // 2 % 2], 16)

            run_slots(sp, slot)
            for n in range(2):
                sp.wait_ge(stored[n], 16 * ((tiles + 2 - n) // 2))

        @block.gpsimd
        def _(pool):
            nc.gpsimd.memset(zeros[:, :], 0.0).then_inc(constants, 1)
            nc.gpsimd.memset(eps[:, :], EPS).then_inc(constants, 1)
            nc.gpsimd.iota(lane_i[:, :], pattern=[[0, 1]], base=nodes, channel_multiplier=1
                           ).then_inc(constants, 1)
            nc.gpsimd.memset(identity[:, :], 0.0).then_inc(masks_cleared, 1)
            nc.gpsimd.memset(earlier[:, :], 0.0).then_inc(masks_cleared, 1)
            pool.wait_ge(masks_cleared, 2)
            nc.gpsimd.affine_select(out=identity[:, :], in_=identity[:, :], compare_op=ALU.not_equal,
                                    fill=1.0, base=0, pattern=[[-1, LANES]], channel_multiplier=1
                                    ).then_inc(constants, 1)
            nc.gpsimd.affine_select(out=earlier[:, :], in_=earlier[:, :], compare_op=ALU.is_ge,
                                    fill=1.0, base=0, pattern=[[1, LANES]], channel_multiplier=-1
                                    ).then_inc(constants, 1)
            pool.wait_ge(biases_loaded, 48)
            pool.wait_ge(dst_loaded, 32)

            def add_bias3(step):
                P, J = lanes(step.c), subs(step.c)
                if is_edge_step(step):
                    f = step - FIRST_EDGE
                    reached(pool, x_gathered[step.slot(RING)], f.turns(RING, 16 * SUB, 16 * J))
                else:
                    reached(pool, x_loaded[step.c // 2 % 2], step.turns(4, 16, 16))
                reached(pool, y_summed, step.count(plus=-RING + 1))
                nc.gpsimd.tensor_tensor(
                    xb3[0:P, step.slot(RING), 0:J, :], xin[0:P, step.c // 2 % 2, step.c % 2, 0:J, :],
                    bias3[0:P, :].unsqueeze(1).to_broadcast([P, J, D]), ALU.add
                ).then_inc(xb3_done, 1)

            def apart():
                pool.sem_inc(pool_passed, 1)

            def list_rows(to, semaphore, of, group, half, P, J):
                apart()
                nc.gpsimd.tensor_copy(to[0:P, half, 0:J],
                                      of[0:P, bass.ds(group * SUB, J)]).then_inc(semaphore, 1)
                reached(pool, semaphore, group + 1)
                apart()

            add_bias3(Step(0, 0))

            def slot(s):
                if exists(s + 1):
                    add_bias3(s + 1)
                if now := pair_of(s):
                    pair, group, P, j0, J = now
                    if pair.c == 0:
                        pool.wait_ge(cleared, 16 * CLEARS)
                    reached(pool, added, pair.count(32))
                    if j0 == 0:
                        list_rows(add_at, add_at_set, own_i, group, pair.c // 2 % 2, P, J)
                    reached(pool, sums_copied, pair.count(plus=1))
                    for j in range(2):
                        reached(pool, added, pair.count(32, 16 * j))
                        apart()
                        nc.gpsimd.indirect_dma_start(
                            out=table[:, :], in_=sums[0:P, pair.slot(2), j, :], in_offset=None,
                            out_offset=bass.IndirectOffsetOnAxis(
                                ap=add_at[0:P, pair.c // 2 % 2, j0 + j:j0 + j + 1], axis=0),
                            compute_op=ALU.add).then_inc(added, 16)
                if is_edge_step(s + 3):
                    step, f = s + 3, s + 3 - FIRST_EDGE
                    P, J = lanes(step.c), subs(step.c)
                    reached(pool, x_transposed, step.count(plus=-3))
                    reached(pool, xb3_done, step.count(plus=-3))
                    if f.c >= 2:
                        reached(pool, x_gathered[(step - 2).slot(RING)],
                                (f - 2).turns(RING, 16 * SUB, 16 * SUB))
                    list_rows(x_from, x_from_set, dst_i, f.count(), f.slot(2), P, J)
                    for j in range(J):
                        nc.gpsimd.indirect_dma_start(
                            out=xin[0:P, step.c // 2 % 2, step.c % 2, j, :], out_offset=None,
                            in_=x[:, :], in_offset=bass.IndirectOffsetOnAxis(
                                ap=x_from[0:P, f.slot(2), j:j + 1], axis=0)
                        ).then_inc(x_gathered[step.slot(RING)], 16)
                if is_edge_step(s + 2):
                    f = s + 2 - FIRST_EDGE
                    P, J = lanes(s.c + 2), subs(s.c + 2)
                    if f.c == 0:
                        pool.wait_ge(added, 16 * CHUNKS)
                    reached(pool, aggr_transposed, f.count(plus=-1))
                    list_rows(aggr_from, aggr_from_set, dst_i, f.count(), f.slot(2), P, J)
                    for j in range(J):
                        nc.gpsimd.indirect_dma_start(
                            out=aggr[0:P, f.slot(2), j, :], out_offset=None,
                            in_=table[:, :], in_offset=bass.IndirectOffsetOnAxis(
                                ap=aggr_from[0:P, f.slot(2), j:j + 1], axis=0)
                        ).then_inc(aggr_gathered[f.slot(2)], 16)
                if is_edge_step(s - 3):
                    step, f = s - 3, s - 3 - FIRST_EDGE
                    P, J = lanes(step.c), subs(step.c)
                    if f.c == 0:
                        for n in range(2):
                            pool.wait_ge(stored[n], 16 * ((tiles + 2 - n) // 2))
                    reached(pool, y_done, step.count(plus=1))
                    if f.c >= 1:
                        reached(pool, scattered[(step - 1).slot(RING)],
                                (f - 1).turns(RING, 16 * SUB, 16 * SUB))
                    list_rows(out_at, out_at_set, out_i, f.count(), f.slot(2), P, J)
                    for j in range(J):
                        nc.gpsimd.indirect_dma_start(
                            out=out[:, :], in_=y[0:P, step.c // 2 % 2, step.c % 2, j, :],
                            in_offset=None, out_offset=bass.IndirectOffsetOnAxis(
                                ap=out_at[0:P, f.slot(2), j:j + 1], axis=0),
                            bounds_check=nodes - 1, oob_is_err=False
                        ).then_inc(scattered[step.slot(RING)], 16)

            run_slots(pool, slot)
            for n in range(RING):
                uses = [c for c in range(FIRST_EDGE, STEPS) if c % RING == n]
                pool.wait_ge(scattered[n], 16 * sum(subs(c) for c in uses))

        @block.scalar
        def _(act):
            act.wait_ge(weights_loaded, 16 * len(raw))
            for name in raw:
                nc.scalar.copy(w_hi[name][:, :, :], raw[name][:, :, :]).then_inc(weights_high, 1)
            act.wait_ge(biases_loaded, 48)
            act.wait_ge(constants, 5)

            def high_of_x(step):
                N = lanes(step.c) * subs(step.c)
                reached(act, x_transposed, step.count(plus=1))
                nc.scalar.copy(x_hi[:, :, 0:N], xT[:, :, 0:N]).then_inc(x_high, 1)

            def relu_of(step, z, bias, kept, hi, z_done, relu_done, high_done, split_done):
                N = lanes(step.c) * subs(step.c)
                reached(act, split_done, step.count())
                for m in range(KD):
                    reached(act, z_done, step.count(KD, m + 1))
                    nc.scalar.activation(kept[:, m, 0:N], z[:, m, 0:N], ACT.Relu,
                                         bias=bias[:, m:m + 1]).then_inc(relu_done, 1)
                    nc.scalar.activation(hi[:, step.slot(2), m, 0:N], z[:, m, 0:N], ACT.Relu,
                                         bias=bias[:, m:m + 1]).then_inc(high_done, 1)

            high_of_x(Step(0, 0))

            def slot(s):
                if exists(s):
                    relu_of(s, z1, bias1, h[:, 0], h1_hi, z1_done, h1_relu, h1_high, h1_split)
                if exists(s + 1):
                    high_of_x(s + 1)
                if exists(s - 3):
                    step = s - 3
                    P, J = lanes(step.c), subs(step.c)
                    reached(act, mean_var_done, step.count(SUB, J))
                    nc.scalar.activation(std[0:P, step.slot(2), 0:J],
                                         mean_var[0:P, step.slot(2), 0:J, 1], ACT.Sqrt,
                                         bias=eps[0:P, :]).then_inc(std_done, 1)
                if exists(s - 1):
                    relu_of(s - 1, z2, bias2, h[:, 1], h2_hi, z2_done, h2_relu, h2_high, h2_split)
                if now := pair_of(s):
                    pair, _, P, _, _ = now
                    reached(act, sums_done, pair.count(plus=1))
                    reached(act, added, pair.count(32, -32))
                    nc.scalar.copy(sums[0:P, pair.slot(2), :, :],
                                   xT[0:P, 0, :].rearrange("p (j d) -> p j d", j=2)
                                   ).then_inc(sums_copied, 1)
                if is_edge_step(s + 1):
                    f = s + 1 - FIRST_EDGE
                    N = lanes(s.c + 1) * subs(s.c + 1)
                    reached(act, aggr_transposed, f.count(plus=1))
                    nc.scalar.copy(a_hi[:, :, 0:N], xT[:, :, 0:N]).then_inc(aggr_high, 1)

            run_slots(act, slot)

        @block.vector
        def _(dve):
            for n, name in enumerate(raw):
                dve.wait_ge(weights_high, n + 1)
                nc.vector.tensor_tensor(w_lo[name][:, :, :], raw[name][:, :, :],
                                        w_hi[name][:, :, :].bitcast(FP32), ALU.subtract
                                        ).then_inc(weights_split, 1)
            dve.wait_ge(constants, 5)
            dve.wait_ge(dst_loaded, 32)
            nc.vector.tensor_copy(lane[:, :], lane_i[:, :]).then_inc(spare_known, 1)
            nc.vector.tensor_copy(dst_f[:, 0:GROUPS * SUB], dst_i[:, 0:GROUPS * SUB]
                                  ).then_inc(dst_f_known, 1)
            nc.vector.tensor_copy(dst_f[0:edge_lanes, GROUPS * SUB:CHUNKS],
                                  dst_i[0:edge_lanes, GROUPS * SUB:CHUNKS]).then_inc(dst_f_known, 1)
            nc.vector.memset(n_above[:, :], 0.0).then_inc(spare_known, 1)
            dve.wait_ge(spare_known, 2)
            dve.wait_ge(dst_f_known, 2)

            def low_of_x(step):
                N = lanes(step.c) * subs(step.c)
                reached(dve, x_high, step.count(plus=1))
                nc.vector.tensor_tensor(x_lo[:, :, 0:N], xT[:, :, 0:N],
                                        x_hi[:, :, 0:N].bitcast(FP32), ALU.subtract
                                        ).then_inc(x_split, 1)

            def low_of_h(step, kept, hi, lo, relu_done, high_done, split_done):
                N = lanes(step.c) * subs(step.c)
                reached(dve, relu_done, step.count(KD, KD))
                reached(dve, high_done, step.count(KD, KD))
                nc.vector.tensor_tensor(lo[:, step.slot(2), :, 0:N], kept[:, :, 0:N],
                                        hi[:, step.slot(2), :, 0:N].bitcast(FP32), ALU.subtract
                                        ).then_inc(split_done, 1)

            def mark(s, group, P, J):
                reached(dve, dst_row_loaded[group.slot(2)], group.turns(2, 16, 16))
                reached(dve, own_known, group.count())
                for j in range(J):
                    nc.vector.scalar_tensor_tensor(
                        out=before[0:P, j, 0:P], in0=dst_rows_of(group.c, j, P, J),
                        scalar=dst_f[0:P, bass.ds(group.count(SUB, j), 1)], in1=earlier[0:P, 0:P],
                        op0=ALU.is_equal, op1=ALU.mult, accum_out=n_before[0:P, j:j + 1]
                    ).then_inc(n_before_done, 1)
                for j in range(1, J):
                    nc.vector.tensor_scalar(
                        above[0:P, j * (j - 1) // 2:j * (j + 1) // 2, 0:P], dst_rows_of(group.c, slice(0, j), P, J),
                        dst_f[0:P, bass.ds(group.count(SUB, j), 1)], None, ALU.is_equal, ALU.add,
                        accum_out=n_above[0:P, j:j + 1]).then_inc(n_before_done, 1)
                cols = bass.ds(group.count(SUB), J)
                nc.vector.tensor_scalar(to_spare[0:P, 0:J], dst_f[0:P, cols], -1.0, lane[0:P, :],
                                        ALU.mult, ALU.add).then_inc(to_spare_done, 1)
                reached(dve, n_before_done, group.count(2 * SUB - 1, 2 * J - 1))
                nc.vector.tensor_tensor(n_both[0:P, 0:J], n_before[0:P, 0:J], n_above[0:P, 0:J],
                                        ALU.add).then_inc(n_both_done, 1)
                reached(dve, to_spare_done, group.count(plus=1))
                reached(dve, n_both_done, group.count(plus=1))
                for n, found in enumerate((n_before, n_both)):
                    nc.vector.scalar_tensor_tensor(
                        out=shift[0:P, n, 0:J], in0=found[0:P, 0:J], scalar=1.0,
                        in1=to_spare[0:P, 0:J], op0=ALU.min, op1=ALU.mult).then_inc(shift_done, 1)
                for n, rows in enumerate((own_i, out_i)):
                    reached(dve, shift_done, group.count(2, n + 1))
                    last = nc.vector.tensor_tensor(rows[0:P, cols], shift[0:P, n, 0:J],
                                                   dst_f[0:P, cols], ALU.add)
                last.then_inc(own_known, 1)

            low_of_x(Step(0, 0))

            def slot(s):
                if exists(s):
                    low_of_h(s, h[:, 0], h1_hi, h1_lo, h1_relu, h1_high, h1_split)
                if exists(s + 1):
                    low_of_x(s + 1)
                if exists(s - 3):
                    step = s - 3
                    P, J = lanes(step.c), subs(step.c)
                    reached(dve, std_done, step.count(plus=1))
                    reached(dve, y_done, step.count())
                    nc.vector.reciprocal(rstd[0:P, 0:J], std[0:P, step.slot(2), 0:J]
                                         ).then_inc(rstd_done, 1)
                    reached(dve, rstd_done, step.count(plus=1))
                    for j in range(J):
                        rows = y[0:P, step.c // 2 % 2, step.c % 2, j, :]
                        last = nc.vector.tensor_scalar(
                            rows, rows, mean_var[0:P, step.slot(2), j, 0:1], rstd[0:P, j:j + 1],
                            ALU.subtract, ALU.mult)
                    last.then_inc(y_done, 1)
                if exists(s - 1):
                    low_of_h(s - 1, h[:, 1], h2_hi, h2_lo, h2_relu, h2_high, h2_split)
                if now := marking_group(s):
                    mark(s, *now)
                if now := pair_of(s):
                    pair, group, P, j0, J = now
                    gc = pair.c // 2 + GROUPS + 1
                    reached(dve, dst_row_loaded[gc % 2], pair.i * 16 + 16 * (gc // 2 + 1))
                    reached(dve, sums_done, pair.count(plus=-1))
                    for j in range(2):
                        last = nc.vector.tensor_scalar(
                            same[0:P, pair.slot(2), j, 0:P], dst_rows_of(gc, j0 + j, P, J),
                            dst_f[0:P, bass.ds(group * SUB + j0 + j, 1)], None, ALU.is_equal)
                    last.then_inc(same_done, 1)
                if is_edge_step(s + 1):
                    f = s + 1 - FIRST_EDGE
                    N = lanes(s.c + 1) * subs(s.c + 1)
                    reached(dve, aggr_high, f.count(plus=1))
                    nc.vector.tensor_tensor(a_lo[:, :, 0:N], xT[:, :, 0:N],
                                            a_hi[:, :, 0:N].bitcast(FP32), ALU.subtract
                                            ).then_inc(aggr_split, 1)
                if exists(s - 2):
                    step = s - 2
                    P, J = lanes(step.c), subs(step.c)
                    reached(dve, z3_done, step.count(plus=1))
                    reached(dve, xb3_done, step.count(plus=1))
                    if step.c - RING >= FIRST_EDGE:
                        reached(dve, scattered[step.slot(RING)],
                                (step - FIRST_EDGE).turns(RING, 16 * SUB))
                    else:
                        reached(dve, stored[step.c // 2 % 2], step.turns(4, 16))
                    rows = y[0:P, step.c // 2 % 2, step.c % 2, 0:J, :]
                    nc.vector.tensor_tensor(rows, z3[0:P, 0:J, :], xb3[0:P, step.slot(RING), 0:J, :],
                                            ALU.add).then_inc(y_summed, 1)
                    reached(dve, y_summed, step.count(plus=1))
                    reached(dve, mean_var_done, step.count(SUB))
                    for j in range(J):
                        nc.vector.bn_stats(stats[0:P, j, :], rows[:, j, :]).then_inc(stats_done, 1)
                    for j in range(J):
                        reached(dve, stats_done, step.count(SUB, j + 1))
                        dve.sem_inc(dve_passed, 1)
                        nc.vector.bn_aggr(mean_var[0:P, step.slot(2), j, :], stats[0:P, j, :]
                                          ).then_inc(mean_var_done, 1)

            run_slots(dve, slot)

        @block.tensor
        def _(pe):
            pe.wait_ge(constants, 5)

            def transpose(step, of, done):
                P, J = lanes(step.c), subs(step.c)
                for k in range(KD):
                    for j in range(J):
                        last = nc.tensor.transpose(xT[:, k, j * P:(j + 1) * P],
                                                   of[0:P, j, k * LANES:(k + 1) * LANES],
                                                   identity[0:P, 0:P])
                last.then_inc(done, 1)

            def transpose_x(step):
                if is_edge_step(step):
                    f = step - FIRST_EDGE
                    reached(pe, x_gathered[step.slot(RING)],
                            f.turns(RING, 16 * SUB, 16 * subs(step.c)))
                    reached(pe, aggr_split, f.count())
                else:
                    reached(pe, x_loaded[step.c // 2 % 2], step.turns(4, 16, 16))
                    reached(pe, x_split, step.count())
                    if now := pair_of(step - 2):
                        reached(pe, sums_copied, now[0].count(plus=1))
                transpose(step, xin[:, step.c // 2 % 2, step.c % 2, :, :], x_transposed)

            def layer(step, z, operands, done):
                N = lanes(step.c) * subs(step.c)
                for m in range(KD):
                    passes = [(w[:, k, m * LANES:(m + 1) * LANES], v[:, k, 0:N])
                              for name, v_hi, v_lo in operands
                              for w, v in ((w_hi[name], v_hi), (w_lo[name], v_hi),
                                           (w_hi[name], v_lo))
                              for k in range(KD)]
                    for n, (w, v) in enumerate(passes):
                        last = nc.tensor.matmul(z[:, m, 0:N], w, v, start=n == 0,
                                                stop=n == len(passes) - 1)
                    last.then_inc(done, 1)

            transpose_x(Step(0, 0))
            pe.wait_ge(weights_split, len(raw))

            def slot(s):
                if exists(s):
                    reached(pe, x_split, s.count(plus=1))
                    reached(pe, h1_high, s.count(KD))
                    operands = [("w1x", x_hi, x_lo)]
                    if is_edge_step(s):
                        reached(pe, aggr_split, (s - FIRST_EDGE).count(plus=1))
                        operands.append(("w1a", a_hi, a_lo))
                    layer(s, z1, operands, z1_done)
                if exists(s + 1):
                    transpose_x(s + 1)
                if exists(s - 1):
                    step = s - 1
                    reached(pe, h1_split, step.count(plus=1))
                    reached(pe, h2_high, step.count(KD))
                    layer(step, z2, [("w2", h1_hi[:, step.slot(2)], h1_lo[:, step.slot(2)])],
                          z2_done)
                if now := pair_of(s):
                    pair, _, P, j0, _ = now
                    reached(pe, same_done, pair.count(plus=1))
                    reached(pe, e_loaded[pair.c // 2 % 2], pair.turns(4, 16, 16))
                    reached(pe, x_split, s.count(plus=2))
                    for j in range(2):
                        last = nc.tensor.matmul(xT[0:P, 0, j * D:(j + 1) * D],
                                                same[0:P, pair.slot(2), j, 0:P],
                                                e_in[0:P, pair.c // 2 % 2, j0 + j, :],
                                                start=True, stop=True)
                    last.then_inc(sums_done, 1)
                if is_edge_step(s + 1):
                    step, f = s + 1, s + 1 - FIRST_EDGE
                    reached(pe, aggr_gathered[f.slot(2)], f.turns(2, 16 * SUB, 16 * subs(step.c)))
                    reached(pe, x_split, step.count(plus=1))
                    transpose(step, aggr[:, f.slot(2), :, :], aggr_transposed)
                if exists(s - 2):
                    step = s - 2
                    P, J = lanes(step.c), subs(step.c)
                    reached(pe, h2_split, step.count(plus=1))
                    reached(pe, y_summed, step.count())
                    hi, lo = h2_hi[:, step.slot(2)], h2_lo[:, step.slot(2)]
                    for j in range(J):
                        cols = slice(j * P, (j + 1) * P)
                        passes = [(v[:, k, cols], w["w3"][:, k, :])
                                  for v, w in ((hi, w_hi), (hi, w_lo), (lo, w_hi))
                                  for k in range(KD)]
                        for n, (v, w) in enumerate(passes):
                            last = nc.tensor.matmul(z3[0:P, j, :], v, w, start=n == 0,
                                                    stop=n == len(passes) - 1)
                    last.then_inc(z3_done, 1)

            run_slots(pe, slot)


_INS = ['x', 'src', 'dst', 'edge_attr_256', 'L0_gnn_W1', 'L0_gnn_b1', 'L0_gnn_W2', 'L0_gnn_b2',
        'L0_gnn_W3', 'L0_gnn_b3']


def kernel(**inputs):
    import numpy as _np
    import concourse.bacc as _bacc
    from concourse import mybir as _mybir
    from concourse.bass_utils import run_bass_kernel_spmd as _run

    nc = _bacc.Bacc("TRN2", target_bir_lowering=False, num_devices=1)
    arrays, args = {}, []
    for name in _INS:
        a = _np.ascontiguousarray(inputs[name])
        arrays[f"in_{name}_dram"] = a
        args.append(nc.dram_tensor(f"in_{name}_dram", a.shape, _mybir.dt.from_np(a.dtype),
                                   kind="ExternalInput").ap())
    out = nc.dram_tensor("out_0_dram", args[0].shape, _mybir.dt.float32, kind="ExternalOutput").ap()
    bass_gnn_residual_norm(nc, *args, out)
    r = _run(nc, [arrays], core_ids=[0])
    return r.results[0]["out_0_dram"]
```

```python
import concourse.bass as bass
from concourse import mybir
from contextlib import ExitStack

FP32 = mybir.dt.float32
FP32R = mybir.dt.float32r
BF16 = mybir.dt.bfloat16
INT32 = mybir.dt.int32
ALU = mybir.AluOpType
ACT = mybir.ActivationFunctionType

LANES = 128
SUB = 4
STEP = LANES * SUB
RING = 4
ACT_NORMS = 2
EPS = 1e-5


class Step:

    def __init__(self, i, c):
        self.i, self.c = i, c

    def __add__(self, o):
        return Step(self.i, self.c + o)

    def __sub__(self, o):
        return Step(self.i, self.c - o)

    def count(self, per=1, plus=0):
        return self.i * (RING * per) + (self.c * per + plus)

    def turns(self, ring, per=1, plus=0):
        return self.i * (RING // ring * per) + (self.c // ring * per + plus)

    def slot(self, ring):
        return self.c % ring


def reached(engine, semaphore, value):
    if isinstance(value, int) and value <= 0:
        return
    engine.wait_ge(semaphore, value)


def bass_gnn_residual_norm(nc, x, src, dst, edges, w1, b1, w2, b2, w3, b3, out):
    nodes, D = x.shape
    n_edges = edges.shape[0]
    KD = D // LANES

    tiles = nodes // (2 * STEP)
    assert tiles % 2 == 0
    PLAIN = 2 * tiles
    tail_rows = nodes - PLAIN * STEP
    tail_lanes = tail_rows // (2 * SUB)
    assert tail_rows == tail_lanes * 2 * SUB and 0 < tail_lanes <= LANES
    FIRST_EDGE = PLAIN + 2
    GROUPS = n_edges // STEP
    assert GROUPS % RING == 0 and GROUPS >= RING
    edge_tail = n_edges - GROUPS * STEP
    TAIL_SUB = 2
    edge_lanes = edge_tail // TAIL_SUB
    assert edge_tail == edge_lanes * TAIL_SUB and 0 < edge_lanes <= LANES
    CHUNKS = GROUPS * SUB + TAIL_SUB
    STEPS = FIRST_EDGE + GROUPS + 1

    CLEAR = 3 * STEP
    CLEARS = -(-(nodes + LANES) // CLEAR)
    ADD0 = -(-(max(CLEARS, GROUPS) + 2) // RING) * RING
    ADD_END = ADD0 + 2 * GROUPS
    PAIRS = 2 * GROUPS + 1
    assert ADD_END + RING <= PLAIN

    def lanes(c):
        return tail_lanes if PLAIN <= c < FIRST_EDGE else edge_lanes if c == STEPS - 1 else LANES

    def subs(c):
        return TAIL_SUB if c == STEPS - 1 else SUB

    def exists(step):
        return 0 <= step.c < STEPS

    def is_edge_step(step):
        return FIRST_EDGE <= step.c < STEPS

    def is_tail(step):
        return step.c == PLAIN or step.c == PLAIN + 1

    loops = [(2 * RING, min(GROUPS, CLEARS) - RING), (ADD0 + RING, ADD_END - RING),
             (ADD_END + RING, PLAIN - RING), (FIRST_EDGE + 6, FIRST_EDGE + GROUPS - 3)]

    def run_slots(engine, slot):
        at = 0
        for begin, end in loops:
            turns = (end - begin) // RING
            if turns < 1:
                continue
            for c in range(at, begin):
                slot(Step(0, c))
            with engine.Fori(0, turns) as i:
                for k in range(RING):
                    slot(Step(i, begin + k))
            at = begin + turns * RING
        for c in range(at, STEPS + 4):
            slot(Step(0, c))

    x_edge = nc.dram_tensor("x_edge", (n_edges, D), FP32).ap()
    table = nc.dram_tensor("aggr_table", (CLEARS * CLEAR, D), FP32).ap()

    ctx = ExitStack()
    with ctx:
        def sb(name, shape, dt=FP32):
            return ctx.enter_context(nc.sbuf_tensor(name, shape, dt))

        def sem(name):
            return ctx.enter_context(nc.semaphore(name))

        raw = {n: sb(f"raw_{n}", [LANES, KD, D]) for n in ("w1x", "w1a", "w2", "w3")}
        w_hi = {n: sb(f"hi_{n}", [LANES, KD, D], FP32R) for n in raw}
        w_lo = {n: sb(f"lo_{n}", [LANES, KD, D], FP32R) for n in raw}
        bias1 = sb("bias1", [LANES, KD])
        bias2 = sb("bias2", [LANES, KD])
        bias3 = sb("bias3", [LANES, D])
        eps = sb("eps", [LANES, 1])
        zeros = sb("zeros", [LANES, SUB * D])
        identity = sb("identity", [LANES, LANES])
        earlier = sb("earlier", [LANES, LANES])
        lane = sb("lane", [LANES, 1])
        lane_i = sb("lane_i", [LANES, 1], INT32)

        xin = sb("xin", [LANES, 2, 2, SUB, D])
        xb3 = sb("xb3", [LANES, RING, SUB, D])
        y = sb("y", [LANES, 2, 2, SUB, D])
        aggr = sb("aggr", [LANES, 2, SUB, D])
        x_hi = sb("x_hi", [LANES, KD, STEP], FP32R)
        x_lo = sb("x_lo", [LANES, KD, STEP], FP32R)
        a_hi = sb("a_hi", [LANES, KD, STEP], FP32R)
        a_lo = sb("a_lo", [LANES, KD, STEP], FP32R)
        h = sb("h", [LANES, 2, KD, STEP])
        h1_hi = sb("h1_hi", [LANES, 2, KD, STEP], FP32R)
        h1_lo = sb("h1_lo", [LANES, 2, KD, STEP], FP32R)
        h2_hi = sb("h2_hi", [LANES, 2, KD, STEP], FP32R)
        h2_lo = sb("h2_lo", [LANES, 2, KD, STEP], FP32R)
        stats = sb("stats", [LANES, SUB, 6])
        mean_var = sb("mean_var", [LANES, 2, SUB, 2])
        std = sb("std", [LANES, 2, SUB])
        rstd = sb("rstd", [LANES, SUB])
        dst_i = sb("dst_i", [LANES, CHUNKS], INT32)
        dst_f = sb("dst_f", [LANES, CHUNKS])
        own_i = sb("own_i", [LANES, CHUNKS], INT32)
        out_i = sb("out_i", [LANES, CHUNKS], INT32)
        dst_row = sb("dst_row", [LANES, RING, STEP], INT32)
        dst_add = sb("dst_add", [LANES, 2, STEP], INT32)
        e_in = sb("e_in", [LANES, 2, SUB, D])
        same = sb("same", [LANES, 2, 2, LANES])
        sums = sb("sums", [LANES, 2, 2, D])
        before = sb("before", [LANES, SUB, LANES], BF16)
        above = sb("above", [LANES, SUB * (SUB - 1) // 2, LANES], BF16)
        n_before = sb("n_before", [LANES, SUB])
        n_above = sb("n_above", [LANES, SUB])
        to_spare = sb("to_spare", [LANES, 2, SUB])
        shift = sb("shift", [LANES, 2, SUB])
        xg = sb("xg", [LANES, 2, SUB, D])
        minus_mean = sb("minus_mean", [LANES, SUB])
        add_at = sb("add_at", [LANES, 2, SUB], INT32)
        x_from = sb("x_from", [LANES, 2, SUB], INT32)
        aggr_from = sb("aggr_from", [LANES, 2, SUB], INT32)
        out_at = sb("out_at", [LANES, 2, SUB], INT32)

        xT = ctx.enter_context(nc.psum_tensor("xT", [LANES, KD, STEP], FP32))
        z1 = ctx.enter_context(nc.psum_tensor("z1", [LANES, KD, STEP], FP32))
        z2 = ctx.enter_context(nc.psum_tensor("z2", [LANES, KD, STEP], FP32))
        z3 = ctx.enter_context(nc.psum_tensor("z3", [LANES, SUB, D], FP32))

        weights_loaded, biases_loaded = sem("weights_loaded"), sem("biases_loaded")
        dst_loaded = sem("dst_loaded")
        weights_high, weights_split = sem("weights_high"), sem("weights_split")
        constants = sem("constants")
        masks_cleared = sem("masks_cleared")
        spare_known, dst_f_known = sem("spare_known"), sem("dst_f_known")
        x_loaded = [sem(f"x_loaded{n}") for n in range(2)]
        x_fetched = [sem(f"x_fetched{n}") for n in range(2)]
        x_kept = [sem(f"x_kept{n}") for n in range(2)]
        x_edge_loaded = [sem(f"x_edge_loaded{n}") for n in range(RING)]
        aggr_gathered = [sem(f"aggr_gathered{n}") for n in range(2)]
        x_transposed, x_high, x_split = sem("x_transposed"), sem("x_high"), sem("x_split")
        aggr_transposed, aggr_high, aggr_split = (
            sem("aggr_transposed"), sem("aggr_high"), sem("aggr_split"))
        z1_done, h1_relu, h1_high, h1_split = (
            sem("z1_done"), sem("h1_relu"), sem("h1_high"), sem("h1_split"))
        z2_done, h2_relu, h2_high, h2_split = (
            sem("z2_done"), sem("h2_relu"), sem("h2_high"), sem("h2_split"))
        z3_done, xb3_done, y_summed = sem("z3_done"), sem("xb3_done"), sem("y_summed")
        stats_done, mean_var_done = sem("stats_done"), sem("mean_var_done")
        std_done, rstd_done, y_done = sem("std_done"), sem("rstd_done"), sem("y_done")
        bias_done, y_part_done = sem("bias_done"), sem("y_part_done")
        stored = [sem(f"stored{n}") for n in range(2)]
        scattered = [sem(f"scattered{n}") for n in range(RING)]
        dst_row_loaded = [sem(f"dst_row_loaded{n}") for n in range(RING)]
        dst_add_loaded = [sem(f"dst_add_loaded{n}") for n in range(2)]
        e_loaded = [sem(f"e_loaded{n}") for n in range(2)]
        n_before_done, to_spare_done, shift_done, own_known = (
            sem("n_before_done"), sem("to_spare_done"), sem("shift_done"), sem("own_known"))
        n_above_done, out_spare_done, out_shift_done, out_known = (
            sem("n_above_done"), sem("out_spare_done"), sem("out_shift_done"), sem("out_known"))
        cleared = sem("cleared")
        added = sem("added")
        pool_passed, dve_passed = sem("pool_passed"), sem("dve_passed")
        add_at_set, x_from_set, aggr_from_set, out_at_set = (
            sem("add_at_set"), sem("x_from_set"), sem("aggr_from_set"),
            sem("out_at_set"))
        same_done, sums_done, sums_copied = (
            sem("same_done"), sem("sums_done"), sem("sums_copied"))

        block = ctx.enter_context(nc.Block())

        def pair_of(s):
            pair = s - ADD0
            if not 0 <= pair.c < PAIRS:
                return None
            group = pair.turns(2)
            if pair.c == PAIRS - 1:
                return pair, group, edge_lanes, 0, TAIL_SUB
            return pair, group, LANES, 2 * pair.slot(2), SUB

        def marking_group(s):
            if s.c > GROUPS:
                return None
            return (s, edge_lanes, TAIL_SUB) if s.c == GROUPS else (s, LANES, SUB)

        def dst_rows_of(rows, sub, n_lanes, n_sub):
            v = rows[0:n_lanes, 0:n_lanes * n_sub]
            return v.rearrange("q (p j) -> q j p", j=n_sub)[:, sub]

        @block.sync
        def _(sp):
            def load_tile(step):
                n = step.turns(2)
                if is_tail(step):
                    rows = x[PLAIN * STEP:nodes, :].rearrange("(p j) d -> p (j d)", j=2 * SUB)
                    to = xin[0:tail_lanes, step.c // 2 % 2, :, :, :]
                else:
                    rows = x[bass.ds(n * (2 * STEP), 2 * STEP), :].rearrange(
                        "(p j) d -> p (j d)", j=2 * SUB)
                    to = xin[:, step.c // 2 % 2, :, :, :]
                sp.dma_start(to.rearrange("p t j d -> p (t j d)"), rows).then_inc(
                    x_loaded[step.c // 2 % 2], 16)

            def load_dst_row(to, semaphore, group, n_edges_of):
                sp.dma_start(to[:, 0:n_edges_of],
                             dst[bass.ds(group * STEP, n_edges_of)].unsqueeze(0).to_broadcast(
                                 [LANES, n_edges_of])).then_inc(semaphore, 16)

            def load_edges(group_c, group, n_lanes, n_sub):
                sp.dma_start(e_in[0:n_lanes, group_c % 2, 0:n_sub, :].rearrange("p j d -> p (j d)"),
                             edges[bass.ds(group * STEP, n_lanes * n_sub), :].rearrange(
                                 "(p j) d -> p (j d)", j=n_sub)).then_inc(e_loaded[group_c % 2], 16)

            load_tile(Step(0, 0))
            halves = (("w1x", w1[0:D, :]), ("w1a", w1[D:2 * D, :]), ("w2", w2), ("w3", w3))
            for name, w in halves:
                sp.dma_start(raw[name][:, :, :], w.rearrange("(k p) n -> p k n", p=LANES)).then_inc(
                    weights_loaded, 16)
            with nc.allow_non_contiguous_dma(reason="two biases of 256 words, once"):
                for to, b in ((bias1, b1), (bias2, b2)):
                    sp.dma_start(to[:, :], b.rearrange("(k p) -> p k", p=LANES)).then_inc(
                        biases_loaded, 16)
            sp.dma_start(bias3[:, :], b3.unsqueeze(0).to_broadcast([LANES, D])).then_inc(
                biases_loaded, 16)
            sp.dma_start(dst_i[:, 0:GROUPS * SUB].rearrange("p (g j) -> p g j", j=SUB),
                         dst[0:GROUPS * STEP].rearrange("(g p j) -> p g j", p=LANES, j=SUB)
                         ).then_inc(dst_loaded, 16)
            sp.dma_start(dst_i[0:edge_lanes, GROUPS * SUB:CHUNKS],
                         dst[GROUPS * STEP:n_edges].rearrange("(p j) -> p j", j=TAIL_SUB)
                         ).then_inc(dst_loaded, 16)
            for g in range(2):
                load_dst_row(dst_row[:, g, :], dst_row_loaded[g], g, STEP)
            load_tile(Step(0, 2))

            sp.wait_ge(constants, 5)

            def slot(s):
                if s.c < CLEARS:
                    sp.dma_start(table[bass.ds(s.count(CLEAR), CLEAR), :].rearrange(
                        "(p n j) d -> p n (j d)", p=LANES, j=SUB),
                        zeros[:, :].unsqueeze(1).to_broadcast([LANES, CLEAR // STEP, SUB * D])
                    ).then_inc(cleared, 16)
                kept = s - 2 - ADD0
                if 0 <= kept.c < PAIRS and (kept.c % 2 == 1 or kept.c == PAIRS - 1):
                    half = kept.c // 2 % 2
                    P, J = (edge_lanes, TAIL_SUB) if kept.c == PAIRS - 1 else (LANES, SUB)
                    reached(sp, x_fetched[half], kept.turns(4, 16 * SUB, 16 * J))
                    sp.dma_start(x_edge[bass.ds(kept.turns(2) * STEP, P * J), :].rearrange(
                        "(p j) d -> p (j d)", j=J),
                        xg[0:P, half, 0:J, :].rearrange("p j d -> p (j d)")
                    ).then_inc(x_kept[half], 16)
                g = s + 2
                if g.c <= GROUPS:
                    reached(sp, own_known, g.count(plus=-3))
                    load_dst_row(dst_row[:, g.slot(RING), :], dst_row_loaded[g.slot(RING)],
                                 g.count(), edge_tail if g.c == GROUPS else STEP)
                ahead = s + 2 - ADD0
                if ahead.c >= 0 and ahead.c % 2 == 0 and ahead.c < PAIRS:
                    gc, group = ahead.c // 2, ahead.turns(2)
                    last = gc == GROUPS
                    reached(sp, sums_done, ahead.count(plus=-2))
                    reached(sp, out_known, ahead.turns(2, plus=-1))
                    load_dst_row(dst_add[:, gc % 2, :], dst_add_loaded[gc % 2], group,
                                 edge_tail if last else STEP)
                    load_edges(gc, group, edge_lanes if last else LANES, TAIL_SUB if last else SUB)
                if s.c % 2 == 1 and s.c + 3 <= PLAIN:
                    reached(sp, x_transposed, s.count(plus=1))
                    reached(sp, xb3_done, s.count(plus=1))
                    load_tile(s + 3)
                if is_edge_step(s + 3):
                    step, f = s + 3, s + 3 - FIRST_EDGE
                    P, J = lanes(step.c), subs(step.c)
                    if f.c == 0:
                        for n in range(2):
                            sp.wait_ge(x_kept[n], 16 * ((GROUPS + 2 - n) // 2))
                    reached(sp, x_transposed, step.count(plus=-3))
                    reached(sp, xb3_done, step.count(plus=-3))
                    sp.dma_start(xin[0:P, step.c // 2 % 2, step.c % 2, 0:J, :].rearrange(
                        "p j d -> p (j d)"),
                        x_edge[bass.ds(f.count(STEP), P * J), :].rearrange(
                            "(p j) d -> p (j d)", j=J)
                    ).then_inc(x_edge_loaded[step.slot(RING)], 16)
                done = s - 5
                if done.c >= 0 and done.c % 2 == 0 and done.c <= PLAIN:
                    reached(sp, y_done, done.count(plus=2))
                    reached(sp, y_part_done, done.count(plus=2))
                    if is_tail(done):
                        rows = out[PLAIN * STEP:nodes, :].rearrange("(p j) d -> p (j d)", j=2 * SUB)
                        of = y[0:tail_lanes, done.c // 2 % 2, :, :, :]
                    else:
                        rows = out[bass.ds(done.turns(2) * (2 * STEP), 2 * STEP), :].rearrange(
                            "(p j) d -> p (j d)", j=2 * SUB)
                        of = y[:, done.c // 2 % 2, :, :, :]
                    sp.dma_start(rows, of.rearrange("p t j d -> p (t j d)")).then_inc(
                        stored[done.c // 2 % 2], 16)

            run_slots(sp, slot)
            for n in range(2):
                sp.wait_ge(stored[n], 16 * ((tiles + 2 - n) // 2))

        @block.gpsimd
        def _(pool):
            nc.gpsimd.memset(zeros[:, :], 0.0).then_inc(constants, 1)
            nc.gpsimd.memset(eps[:, :], EPS).then_inc(constants, 1)
            nc.gpsimd.iota(lane_i[:, :], pattern=[[0, 1]], base=nodes, channel_multiplier=1
                           ).then_inc(constants, 1)
            nc.gpsimd.memset(identity[:, :], 0.0).then_inc(masks_cleared, 1)
            nc.gpsimd.memset(earlier[:, :], 0.0).then_inc(masks_cleared, 1)
            pool.wait_ge(masks_cleared, 2)
            nc.gpsimd.affine_select(out=identity[:, :], in_=identity[:, :], compare_op=ALU.not_equal,
                                    fill=1.0, base=0, pattern=[[-1, LANES]], channel_multiplier=1
                                    ).then_inc(constants, 1)
            nc.gpsimd.affine_select(out=earlier[:, :], in_=earlier[:, :], compare_op=ALU.is_ge,
                                    fill=1.0, base=0, pattern=[[1, LANES]], channel_multiplier=-1
                                    ).then_inc(constants, 1)
            pool.wait_ge(biases_loaded, 48)
            pool.wait_ge(dst_loaded, 32)

            def add_bias3(step):
                P, J = lanes(step.c), subs(step.c)
                if is_edge_step(step):
                    f = step - FIRST_EDGE
                    reached(pool, x_edge_loaded[step.slot(RING)], f.turns(RING, 16, 16))
                else:
                    reached(pool, x_loaded[step.c // 2 % 2], step.turns(4, 16, 16))
                reached(pool, y_summed, step.count(plus=-RING + 1))
                nc.gpsimd.tensor_tensor(
                    xb3[0:P, step.slot(RING), 0:J, :], xin[0:P, step.c // 2 % 2, step.c % 2, 0:J, :],
                    bias3[0:P, :].unsqueeze(1).to_broadcast([P, J, D]), ALU.add
                ).then_inc(xb3_done, 1)

            def apart():
                pool.sem_inc(pool_passed, 1)

            def list_rows(to, semaphore, of, group, half, P, J):
                apart()
                nc.gpsimd.tensor_copy(to[0:P, half, 0:J],
                                      of[0:P, bass.ds(group * SUB, J)]).then_inc(semaphore, 1)
                reached(pool, semaphore, group + 1)
                apart()

            add_bias3(Step(0, 0))

            def slot(s):
                if exists(s + 1):
                    add_bias3(s + 1)
                if now := pair_of(s):
                    pair, group, P, j0, J = now
                    if pair.c == 0:
                        pool.wait_ge(cleared, 16 * CLEARS)
                    half = pair.c // 2 % 2
                    reached(pool, added, pair.count(32))
                    if j0 == 0:
                        list_rows(add_at, add_at_set, own_i, group, half, P, J)
                        reached(pool, x_kept[half], pair.turns(4, 16))
                        list_rows(x_from, x_from_set, dst_i, group, half, P, J)

                    def fetch(j):
                        nc.gpsimd.indirect_dma_start(
                            out=xg[0:P, half, j, :], out_offset=None, in_=x[:, :],
                            in_offset=bass.IndirectOffsetOnAxis(ap=x_from[0:P, half, j:j + 1],
                                                                axis=0)
                        ).then_inc(x_fetched[half], 16)

                    apart()
                    fetch(j0)
                    reached(pool, sums_copied, pair.count(plus=1))
                    for j in range(2):
                        if j == 1:
                            fetch(j0 + 1)
                        reached(pool, added, pair.count(32, 16 * j))
                        apart()
                        nc.gpsimd.indirect_dma_start(
                            out=table[:, :], in_=sums[0:P, pair.slot(2), j, :], in_offset=None,
                            out_offset=bass.IndirectOffsetOnAxis(
                                ap=add_at[0:P, half, j0 + j:j0 + j + 1], axis=0),
                            compute_op=ALU.add).then_inc(added, 16)
                if is_edge_step(s + 2):
                    f = s + 2 - FIRST_EDGE
                    P, J = lanes(s.c + 2), subs(s.c + 2)
                    if f.c == 0:
                        pool.wait_ge(added, 16 * CHUNKS)
                    reached(pool, aggr_transposed, f.count(plus=-1))
                    list_rows(aggr_from, aggr_from_set, dst_i, f.count(), f.slot(2), P, J)
                    for j in range(J):
                        nc.gpsimd.indirect_dma_start(
                            out=aggr[0:P, f.slot(2), j, :], out_offset=None,
                            in_=table[:, :], in_offset=bass.IndirectOffsetOnAxis(
                                ap=aggr_from[0:P, f.slot(2), j:j + 1], axis=0)
                        ).then_inc(aggr_gathered[f.slot(2)], 16)
                if is_edge_step(s - 4):
                    step, f = s - 4, s - 4 - FIRST_EDGE
                    P, J = lanes(step.c), subs(step.c)
                    if f.c == 0:
                        for n in range(2):
                            pool.wait_ge(stored[n], 16 * ((tiles + 2 - n) // 2))
                    if J > ACT_NORMS:
                        reached(pool, y_done, step.count(plus=1))
                    reached(pool, y_part_done, step.count(plus=1))
                    if f.c >= 1:
                        reached(pool, scattered[(step - 1).slot(RING)],
                                (f - 1).turns(RING, 16 * SUB, 16 * SUB))
                    list_rows(out_at, out_at_set, out_i, f.count(), f.slot(2), P, J)
                    for j in range(J):
                        nc.gpsimd.indirect_dma_start(
                            out=out[:, :], in_=y[0:P, step.c // 2 % 2, step.c % 2, j, :],
                            in_offset=None, out_offset=bass.IndirectOffsetOnAxis(
                                ap=out_at[0:P, f.slot(2), j:j + 1], axis=0),
                            bounds_check=nodes - 1, oob_is_err=False
                        ).then_inc(scattered[step.slot(RING)], 16)

            run_slots(pool, slot)
            for n in range(RING):
                uses = [c for c in range(FIRST_EDGE, STEPS) if c % RING == n]
                pool.wait_ge(scattered[n], 16 * sum(subs(c) for c in uses))

        @block.scalar
        def _(act):
            act.wait_ge(weights_loaded, 16 * len(raw))
            for name in raw:
                nc.scalar.copy(w_hi[name][:, :, :], raw[name][:, :, :]).then_inc(weights_high, 1)
            act.wait_ge(biases_loaded, 48)
            act.wait_ge(constants, 5)

            def high_of_x(step):
                N = lanes(step.c) * subs(step.c)
                reached(act, x_transposed, step.count(plus=1))
                nc.scalar.copy(x_hi[:, :, 0:N], xT[:, :, 0:N]).then_inc(x_high, 1)

            def relu_of(step, z, bias, kept, hi, z_done, relu_done, high_done, split_done):
                N = lanes(step.c) * subs(step.c)
                reached(act, split_done, step.count())
                for m in range(KD):
                    reached(act, z_done, step.count(KD, m + 1))
                    nc.scalar.activation(kept[:, m, 0:N], z[:, m, 0:N], ACT.Relu,
                                         bias=bias[:, m:m + 1]).then_inc(relu_done, 1)
                    nc.scalar.activation(hi[:, step.slot(2), m, 0:N], z[:, m, 0:N], ACT.Relu,
                                         bias=bias[:, m:m + 1]).then_inc(high_done, 1)

            high_of_x(Step(0, 0))

            def slot(s):
                if exists(s):
                    relu_of(s, z1, bias1, h[:, 0], h1_hi, z1_done, h1_relu, h1_high, h1_split)
                if exists(s + 1):
                    high_of_x(s + 1)
                if exists(s - 1):
                    relu_of(s - 1, z2, bias2, h[:, 1], h2_hi, z2_done, h2_relu, h2_high, h2_split)
                if now := pair_of(s):
                    pair, _, P, _, _ = now
                    reached(act, sums_done, pair.count(plus=1))
                    reached(act, added, pair.count(32, -32))
                    nc.scalar.copy(sums[0:P, pair.slot(2), :, :],
                                   xT[0:P, 0, :].rearrange("p (j d) -> p j d", j=2)
                                   ).then_inc(sums_copied, 1)
                if is_edge_step(s + 1):
                    f = s + 1 - FIRST_EDGE
                    N = lanes(s.c + 1) * subs(s.c + 1)
                    reached(act, aggr_transposed, f.count(plus=1))
                    nc.scalar.copy(a_hi[:, :, 0:N], xT[:, :, 0:N]).then_inc(aggr_high, 1)

                if exists(s - 3):
                    step = s - 3
                    P, J = lanes(step.c), subs(step.c)
                    reached(act, mean_var_done, step.count(SUB, J))
                    nc.scalar.activation(std[0:P, step.slot(2), 0:J],
                                         mean_var[0:P, step.slot(2), 0:J, 1], ACT.Sqrt,
                                         bias=eps[0:P, :]).then_inc(std_done, 1)
                if exists(s - 4):
                    step = s - 4
                    P, J = lanes(step.c), subs(step.c)
                    reached(act, bias_done, step.count(plus=1))
                    for j in range(J - ACT_NORMS, J):
                        rows = y[0:P, step.c // 2 % 2, step.c % 2, j, :]
                        last = nc.scalar.activation(rows, rows, ACT.Identity,
                                                    bias=minus_mean[0:P, j:j + 1],
                                                    scale=rstd[0:P, j:j + 1])
                    last.then_inc(y_part_done, 1)

            run_slots(act, slot)

        @block.vector
        def _(dve):
            for n, name in enumerate(raw):
                dve.wait_ge(weights_high, n + 1)
                nc.vector.tensor_tensor(w_lo[name][:, :, :], raw[name][:, :, :],
                                        w_hi[name][:, :, :].bitcast(FP32), ALU.subtract
                                        ).then_inc(weights_split, 1)
            dve.wait_ge(constants, 5)
            dve.wait_ge(dst_loaded, 32)
            nc.vector.tensor_copy(lane[:, :], lane_i[:, :]).then_inc(spare_known, 1)
            nc.vector.tensor_copy(dst_f[:, 0:GROUPS * SUB], dst_i[:, 0:GROUPS * SUB]
                                  ).then_inc(dst_f_known, 1)
            nc.vector.tensor_copy(dst_f[0:edge_lanes, GROUPS * SUB:CHUNKS],
                                  dst_i[0:edge_lanes, GROUPS * SUB:CHUNKS]).then_inc(dst_f_known, 1)
            nc.vector.memset(n_above[:, :], 0.0).then_inc(spare_known, 1)
            dve.wait_ge(spare_known, 2)
            dve.wait_ge(dst_f_known, 2)

            def low_of_x(step):
                N = lanes(step.c) * subs(step.c)
                reached(dve, x_high, step.count(plus=1))
                nc.vector.tensor_tensor(x_lo[:, :, 0:N], xT[:, :, 0:N],
                                        x_hi[:, :, 0:N].bitcast(FP32), ALU.subtract
                                        ).then_inc(x_split, 1)

            def low_of_h(step, kept, hi, lo, relu_done, high_done, split_done):
                N = lanes(step.c) * subs(step.c)
                reached(dve, relu_done, step.count(KD, KD))
                reached(dve, high_done, step.count(KD, KD))
                nc.vector.tensor_tensor(lo[:, step.slot(2), :, 0:N], kept[:, :, 0:N],
                                        hi[:, step.slot(2), :, 0:N].bitcast(FP32), ALU.subtract
                                        ).then_inc(split_done, 1)

            def mark(s, group, P, J):
                reached(dve, dst_row_loaded[group.slot(RING)], group.turns(RING, 16, 16))
                reached(dve, own_known, group.count())
                for j in range(J):
                    nc.vector.scalar_tensor_tensor(
                        out=before[0:P, j, 0:P], in0=dst_rows_of(dst_row[:, group.slot(RING), :], j, P, J),
                        scalar=dst_f[0:P, bass.ds(group.count(SUB, j), 1)], in1=earlier[0:P, 0:P],
                        op0=ALU.is_equal, op1=ALU.mult, accum_out=n_before[0:P, j:j + 1]
                    ).then_inc(n_before_done, 1)
                cols = bass.ds(group.count(SUB), J)
                nc.vector.tensor_scalar(to_spare[0:P, 0, 0:J], dst_f[0:P, cols], -1.0, lane[0:P, :],
                                        ALU.mult, ALU.add).then_inc(to_spare_done, 1)
                reached(dve, n_before_done, group.count(SUB, J))
                reached(dve, to_spare_done, group.count(plus=1))
                nc.vector.scalar_tensor_tensor(
                    out=shift[0:P, 0, 0:J], in0=n_before[0:P, 0:J], scalar=1.0,
                    in1=to_spare[0:P, 0, 0:J], op0=ALU.min, op1=ALU.mult).then_inc(shift_done, 1)
                reached(dve, shift_done, group.count(plus=1))
                nc.vector.tensor_tensor(own_i[0:P, cols], shift[0:P, 0, 0:J], dst_f[0:P, cols],
                                        ALU.add).then_inc(own_known, 1)

            def mark_out(group_c, group, P, J):
                reached(dve, out_known, group)
                for j in range(1, J):
                    nc.vector.tensor_scalar(
                        above[0:P, j * (j - 1) // 2:j * (j + 1) // 2, 0:P],
                        dst_rows_of(dst_add[:, group_c % 2, :], slice(0, j), P, J),
                        dst_f[0:P, bass.ds(group * SUB + j, 1)], None, ALU.is_equal, ALU.add,
                        accum_out=n_above[0:P, j:j + 1]).then_inc(n_above_done, 1)
                cols = bass.ds(group * SUB, J)
                nc.vector.tensor_scalar(to_spare[0:P, 1, 0:J], own_i[0:P, cols], -1.0, lane[0:P, :],
                                        ALU.mult, ALU.add).then_inc(out_spare_done, 1)
                reached(dve, n_above_done, group * (SUB - 1) + (J - 1))
                reached(dve, out_spare_done, group + 1)
                nc.vector.scalar_tensor_tensor(
                    out=shift[0:P, 1, 0:J], in0=n_above[0:P, 0:J], scalar=1.0,
                    in1=to_spare[0:P, 1, 0:J], op0=ALU.min, op1=ALU.mult).then_inc(out_shift_done, 1)
                reached(dve, out_shift_done, group + 1)
                nc.vector.tensor_tensor(out_i[0:P, cols], shift[0:P, 1, 0:J], own_i[0:P, cols],
                                        ALU.add).then_inc(out_known, 1)

            low_of_x(Step(0, 0))

            def slot(s):
                if exists(s + 1):
                    low_of_x(s + 1)
                if exists(s):
                    low_of_h(s, h[:, 0], h1_hi, h1_lo, h1_relu, h1_high, h1_split)
                if now := marking_group(s):
                    mark(s, *now)
                if now := pair_of(s):
                    pair, group, P, j0, J = now
                    gc = pair.c // 2
                    reached(dve, dst_add_loaded[gc % 2], pair.turns(4, 16, 16))
                    reached(dve, sums_done, pair.count(plus=-1))
                    for j in range(2):
                        last = nc.vector.tensor_scalar(
                            same[0:P, pair.slot(2), j, 0:P], dst_rows_of(dst_add[:, gc % 2, :], j0 + j, P, J),
                            dst_f[0:P, bass.ds(group * SUB + j0 + j, 1)], None, ALU.is_equal)
                    last.then_inc(same_done, 1)
                    if pair.c % 2 == 1 or pair.c == PAIRS - 1:
                        mark_out(gc, group, P, J)
                if exists(s - 4):
                    step = s - 4
                    P, J = lanes(step.c), subs(step.c)
                    reached(dve, std_done, step.count(plus=1))
                    reached(dve, y_done, step.count())
                    reached(dve, y_part_done, step.count())
                    nc.vector.reciprocal(rstd[0:P, 0:J], std[0:P, step.slot(2), 0:J]
                                         ).then_inc(rstd_done, 1)
                    reached(dve, rstd_done, step.count(plus=1))
                    nc.vector.scalar_tensor_tensor(
                        out=minus_mean[0:P, 0:J], in0=mean_var[0:P, step.slot(2), 0:J, 0],
                        scalar=-1.0, in1=rstd[0:P, 0:J], op0=ALU.mult, op1=ALU.mult
                    ).then_inc(bias_done, 1)
                    for j in range(J - ACT_NORMS):
                        rows = y[0:P, step.c // 2 % 2, step.c % 2, j, :]
                        last = nc.vector.tensor_scalar(
                            rows, rows, mean_var[0:P, step.slot(2), j, 0:1], rstd[0:P, j:j + 1],
                            ALU.subtract, ALU.mult)
                    if J > ACT_NORMS:
                        last.then_inc(y_done, 1)
                if is_edge_step(s + 1):
                    f = s + 1 - FIRST_EDGE
                    N = lanes(s.c + 1) * subs(s.c + 1)
                    reached(dve, aggr_high, f.count(plus=1))
                    nc.vector.tensor_tensor(a_lo[:, :, 0:N], xT[:, :, 0:N],
                                            a_hi[:, :, 0:N].bitcast(FP32), ALU.subtract
                                            ).then_inc(aggr_split, 1)
                if exists(s - 1):
                    low_of_h(s - 1, h[:, 1], h2_hi, h2_lo, h2_relu, h2_high, h2_split)
                if exists(s - 2):
                    step = s - 2
                    P, J = lanes(step.c), subs(step.c)
                    reached(dve, z3_done, step.count(plus=1))
                    reached(dve, xb3_done, step.count(plus=1))
                    if step.c - RING >= FIRST_EDGE:
                        reached(dve, scattered[step.slot(RING)],
                                (step - FIRST_EDGE).turns(RING, 16 * SUB))
                    else:
                        reached(dve, stored[step.c // 2 % 2], step.turns(4, 16))
                    rows = y[0:P, step.c // 2 % 2, step.c % 2, 0:J, :]
                    nc.vector.tensor_tensor(rows, z3[0:P, 0:J, :], xb3[0:P, step.slot(RING), 0:J, :],
                                            ALU.add).then_inc(y_summed, 1)
                    reached(dve, y_summed, step.count(plus=1))
                    reached(dve, mean_var_done, step.count(SUB))
                    for j in range(J):
                        nc.vector.bn_stats(stats[0:P, j, :], rows[:, j, :]).then_inc(stats_done, 1)
                    for j in range(J):
                        reached(dve, stats_done, step.count(SUB, j + 1))
                        dve.sem_inc(dve_passed, 1)
                        nc.vector.bn_aggr(mean_var[0:P, step.slot(2), j, :], stats[0:P, j, :]
                                          ).then_inc(mean_var_done, 1)

            run_slots(dve, slot)

        @block.tensor
        def _(pe):
            pe.wait_ge(constants, 5)

            def transpose(step, of, done):
                P, J = lanes(step.c), subs(step.c)
                for k in range(KD):
                    for j in range(J):
                        last = nc.tensor.transpose(xT[:, k, j * P:(j + 1) * P],
                                                   of[0:P, j, k * LANES:(k + 1) * LANES],
                                                   identity[0:P, 0:P])
                last.then_inc(done, 1)

            def transpose_x(step):
                if is_edge_step(step):
                    f = step - FIRST_EDGE
                    reached(pe, x_edge_loaded[step.slot(RING)], f.turns(RING, 16, 16))
                    reached(pe, aggr_split, f.count())
                else:
                    reached(pe, x_loaded[step.c // 2 % 2], step.turns(4, 16, 16))
                    reached(pe, x_split, step.count())
                    if now := pair_of(step - 2):
                        reached(pe, sums_copied, now[0].count(plus=1))
                transpose(step, xin[:, step.c // 2 % 2, step.c % 2, :, :], x_transposed)

            def layer(step, z, operands, done):
                N = lanes(step.c) * subs(step.c)
                for m in range(KD):
                    passes = [(w[:, k, m * LANES:(m + 1) * LANES], v[:, k, 0:N])
                              for name, v_hi, v_lo in operands
                              for w, v in ((w_hi[name], v_hi), (w_lo[name], v_hi),
                                           (w_hi[name], v_lo))
                              for k in range(KD)]
                    for n, (w, v) in enumerate(passes):
                        last = nc.tensor.matmul(z[:, m, 0:N], w, v, start=n == 0,
                                                stop=n == len(passes) - 1)
                    last.then_inc(done, 1)

            transpose_x(Step(0, 0))
            pe.wait_ge(weights_split, len(raw))

            def slot(s):
                if exists(s):
                    reached(pe, x_split, s.count(plus=1))
                    reached(pe, h1_high, s.count(KD))
                    operands = [("w1x", x_hi, x_lo)]
                    if is_edge_step(s):
                        reached(pe, aggr_split, (s - FIRST_EDGE).count(plus=1))
                        operands.append(("w1a", a_hi, a_lo))
                    layer(s, z1, operands, z1_done)
                if exists(s + 1):
                    transpose_x(s + 1)
                if exists(s - 1):
                    step = s - 1
                    reached(pe, h1_split, step.count(plus=1))
                    reached(pe, h2_high, step.count(KD))
                    layer(step, z2, [("w2", h1_hi[:, step.slot(2)], h1_lo[:, step.slot(2)])],
                          z2_done)
                if is_edge_step(s + 1):
                    step, f = s + 1, s + 1 - FIRST_EDGE
                    reached(pe, aggr_gathered[f.slot(2)], f.turns(2, 16 * SUB, 16 * subs(step.c)))
                    reached(pe, x_split, step.count(plus=1))
                    transpose(step, aggr[:, f.slot(2), :, :], aggr_transposed)
                if exists(s - 2):
                    step = s - 2
                    P, J = lanes(step.c), subs(step.c)
                    reached(pe, h2_split, step.count(plus=1))
                    reached(pe, y_summed, step.count())
                    hi, lo = h2_hi[:, step.slot(2)], h2_lo[:, step.slot(2)]
                    for j in range(J):
                        cols = slice(j * P, (j + 1) * P)
                        passes = [(v[:, k, cols], w["w3"][:, k, :])
                                  for v, w in ((hi, w_hi), (hi, w_lo), (lo, w_hi))
                                  for k in range(KD)]
                        for n, (v, w) in enumerate(passes):
                            last = nc.tensor.matmul(z3[0:P, j, :], v, w, start=n == 0,
                                                    stop=n == len(passes) - 1)
                    last.then_inc(z3_done, 1)
                if now := pair_of(s):
                    pair, _, P, j0, _ = now
                    reached(pe, same_done, pair.count(plus=1))
                    reached(pe, e_loaded[pair.c // 2 % 2], pair.turns(4, 16, 16))
                    reached(pe, x_split, s.count(plus=2))
                    for j in range(2):
                        last = nc.tensor.matmul(xT[0:P, 0, j * D:(j + 1) * D],
                                                same[0:P, pair.slot(2), j, 0:P],
                                                e_in[0:P, pair.c // 2 % 2, j0 + j, :],
                                                start=True, stop=True)
                    last.then_inc(sums_done, 1)

            run_slots(pe, slot)


_INS = ['x', 'src', 'dst', 'edge_attr_256', 'L0_gnn_W1', 'L0_gnn_b1', 'L0_gnn_W2', 'L0_gnn_b2',
        'L0_gnn_W3', 'L0_gnn_b3']


def kernel(**inputs):
    import numpy as _np
    import concourse.bacc as _bacc
    from concourse import mybir as _mybir
    from concourse.bass_utils import run_bass_kernel_spmd as _run

    nc = _bacc.Bacc("TRN2", target_bir_lowering=False, num_devices=1)
    arrays, args = {}, []
    for name in _INS:
        a = _np.ascontiguousarray(inputs[name])
        arrays[f"in_{name}_dram"] = a
        args.append(nc.dram_tensor(f"in_{name}_dram", a.shape, _mybir.dt.from_np(a.dtype),
                                   kind="ExternalInput").ap())
    out = nc.dram_tensor("out_0_dram", args[0].shape, _mybir.dt.float32, kind="ExternalOutput").ap()
    bass_gnn_residual_norm(nc, *args, out)
    r = _run(nc, [arrays], core_ids=[0])
    return r.results[0]["out_0_dram"]
```

```python
import concourse.bass as bass
from concourse import mybir
from contextlib import ExitStack

FP32 = mybir.dt.float32
FP32R = mybir.dt.float32r
BF16 = mybir.dt.bfloat16
INT32 = mybir.dt.int32
ALU = mybir.AluOpType
ACT = mybir.ActivationFunctionType

LANES = 128
SUB = 4
STEP = LANES * SUB
RING = 4
EPS = 1e-5


class Step:

    def __init__(self, i, c):
        self.i, self.c = i, c

    def __add__(self, o):
        return Step(self.i, self.c + o)

    def __sub__(self, o):
        return Step(self.i, self.c - o)

    def count(self, per=1, plus=0):
        return self.i * (RING * per) + (self.c * per + plus)

    def turns(self, ring, per=1, plus=0):
        return self.i * (RING // ring * per) + (self.c // ring * per + plus)

    def slot(self, ring):
        return self.c % ring


def reached(engine, semaphore, value):
    if isinstance(value, int) and value <= 0:
        return
    engine.wait_ge(semaphore, value)


def bass_gnn_residual_norm(nc, x, src, dst, edges, w1, b1, w2, b2, w3, b3, out):
    nodes, D = x.shape
    n_edges = edges.shape[0]
    KD = D // LANES

    tiles = nodes // (2 * STEP)
    assert tiles % 2 == 0
    PLAIN = 2 * tiles
    tail_rows = nodes - PLAIN * STEP
    tail_lanes = tail_rows // (2 * SUB)
    assert tail_rows == tail_lanes * 2 * SUB and 0 < tail_lanes <= LANES
    FIRST_EDGE = PLAIN + 2
    GROUPS = n_edges // STEP
    assert GROUPS % RING == 0 and GROUPS >= RING
    edge_tail = n_edges - GROUPS * STEP
    TAIL_SUB = 2
    edge_lanes = edge_tail // TAIL_SUB
    assert edge_tail == edge_lanes * TAIL_SUB and 0 < edge_lanes <= LANES
    CHUNKS = GROUPS * SUB + TAIL_SUB
    STEPS = FIRST_EDGE + GROUPS + 1

    ZERO_SUB, CLEAR_RUNS = 2, 5
    CLEAR = LANES * ZERO_SUB * CLEAR_RUNS
    CLEARS = -(-(nodes + LANES) // CLEAR)
    ADD0 = -(-(max(CLEARS, GROUPS) + 2) // RING) * RING
    ADD_END = ADD0 + 2 * GROUPS
    PAIRS = 2 * GROUPS + 1
    assert ADD_END + RING <= PLAIN

    def lanes(c):
        return tail_lanes if PLAIN <= c < FIRST_EDGE else edge_lanes if c == STEPS - 1 else LANES

    def subs(c):
        return TAIL_SUB if c == STEPS - 1 else SUB

    def act_norms(step):
        return 3 if step.c + 3 <= GROUPS else 2

    def exists(step):
        return 0 <= step.c < STEPS

    def is_edge_step(step):
        return FIRST_EDGE <= step.c < STEPS

    def is_tail(step):
        return step.c == PLAIN or step.c == PLAIN + 1

    loops = [(2 * RING, min(GROUPS, CLEARS) - RING), (GROUPS + RING, min(CLEARS, ADD0 - 2)),
             (ADD0 + RING, ADD_END - RING), (ADD_END + RING, PLAIN - RING),
             (FIRST_EDGE + 6, FIRST_EDGE + GROUPS - 3)]

    def run_slots(engine, slot):
        at = 0
        for begin, end in loops:
            turns = (end - begin) // RING
            if turns < 1:
                continue
            for c in range(at, begin):
                slot(Step(0, c))
            with engine.Fori(0, turns) as i:
                for k in range(RING):
                    slot(Step(i, begin + k))
            at = begin + turns * RING
        for c in range(at, STEPS + 3):
            slot(Step(0, c))

    x_edge = nc.dram_tensor("x_edge", (n_edges, D), FP32).ap()
    table = nc.dram_tensor("aggr_table", (CLEARS * CLEAR, D), FP32).ap()

    ctx = ExitStack()
    with ctx:
        def sb(name, shape, dt=FP32):
            return ctx.enter_context(nc.sbuf_tensor(name, shape, dt))

        def sem(name):
            return ctx.enter_context(nc.semaphore(name))

        raw = {n: sb(f"raw_{n}", [LANES, KD, D]) for n in ("w1x", "w2", "w3", "w1a")}
        w_hi = {n: sb(f"hi_{n}", [LANES, KD, D], FP32R) for n in raw}
        w_lo = {n: sb(f"lo_{n}", [LANES, KD, D], FP32R) for n in raw}
        bias1 = sb("bias1", [LANES, KD])
        bias2 = sb("bias2", [LANES, KD])
        bias3 = sb("bias3", [LANES, D])
        eps = sb("eps", [LANES, 1])
        zeros = sb("zeros", [LANES, ZERO_SUB * D])
        identity = sb("identity", [LANES, LANES])
        earlier = sb("earlier", [LANES, LANES])
        lane = sb("lane", [LANES, 1])
        lane_i = sb("lane_i", [LANES, 1], INT32)

        xin = sb("xin", [LANES, 2, 2, SUB, D])
        xb3 = sb("xb3", [LANES, RING, SUB, D])
        y = sb("y", [LANES, 2, 2, SUB, D])
        aggr = sb("aggr", [LANES, 2, SUB, D])
        x_hi = sb("x_hi", [LANES, KD, STEP], FP32R)
        x_lo = sb("x_lo", [LANES, KD, STEP], FP32R)
        a_hi = sb("a_hi", [LANES, KD, STEP], FP32R)
        a_lo = sb("a_lo", [LANES, KD, STEP], FP32R)
        h = sb("h", [LANES, 2, KD, STEP])
        h1_hi = sb("h1_hi", [LANES, 2, KD, STEP], FP32R)
        h1_lo = sb("h1_lo", [LANES, 2, KD, STEP], FP32R)
        h2_hi = sb("h2_hi", [LANES, 2, KD, STEP], FP32R)
        h2_lo = sb("h2_lo", [LANES, 2, KD, STEP], FP32R)
        stats = sb("stats", [LANES, SUB, 6])
        mean_var = sb("mean_var", [LANES, 2, SUB, 2])
        std = sb("std", [LANES, 2, SUB])
        rstd = sb("rstd", [LANES, SUB])
        dst_i = sb("dst_i", [LANES, CHUNKS], INT32)
        dst_f = sb("dst_f", [LANES, CHUNKS])
        own_i = sb("own_i", [LANES, CHUNKS], INT32)
        out_i = sb("out_i", [LANES, CHUNKS], INT32)
        dst_row = sb("dst_row", [LANES, RING, STEP], INT32)
        dst_add = sb("dst_add", [LANES, 2, STEP], INT32)
        e_in = sb("e_in", [LANES, 2, SUB, D])
        e_hi = sb("e_hi", [LANES, 2, 2, D], FP32R)
        e_lo = sb("e_lo", [LANES, 2, 2, D], FP32R)
        same = sb("same", [LANES, 2, 2, LANES], FP32R)
        sums = sb("sums", [LANES, 2, 2, D])
        before = sb("before", [LANES, SUB, LANES], BF16)
        above = sb("above", [LANES, SUB * (SUB - 1) // 2, LANES], BF16)
        n_before = sb("n_before", [LANES, SUB])
        n_above = sb("n_above", [LANES, SUB])
        to_spare = sb("to_spare", [LANES, 2, SUB])
        shift = sb("shift", [LANES, 2, SUB])
        xg = sb("xg", [LANES, 2, SUB, D])
        minus_mean = sb("minus_mean", [LANES, SUB])
        add_at = sb("add_at", [LANES, 2, SUB], INT32)
        x_from = sb("x_from", [LANES, 2, SUB], INT32)
        aggr_from = sb("aggr_from", [LANES, 2, SUB], INT32)
        out_at = sb("out_at", [LANES, 2, SUB], INT32)

        xT = ctx.enter_context(nc.psum_tensor("xT", [LANES, KD, STEP], FP32))
        z1 = ctx.enter_context(nc.psum_tensor("z1", [LANES, KD, STEP], FP32))
        z2 = ctx.enter_context(nc.psum_tensor("z2", [LANES, KD, STEP], FP32))
        z3 = ctx.enter_context(nc.psum_tensor("z3", [LANES, SUB, D], FP32))

        weights_loaded = {n: sem(f"{n}_loaded") for n in raw}
        biases_loaded = sem("biases_loaded")
        dst_loaded = sem("dst_loaded")
        weights_high, weights_split = sem("weights_high"), sem("weights_split")
        constants = sem("constants")
        masks_cleared = sem("masks_cleared")
        spare_known, dst_f_known = sem("spare_known"), sem("dst_f_known")
        x_loaded = [sem(f"x_loaded{n}") for n in range(2)]
        x_loaded_first = sem("x_loaded_first")
        x_fetched = [sem(f"x_fetched{n}") for n in range(2)]
        x_kept = [sem(f"x_kept{n}") for n in range(2)]
        x_edge_loaded = [sem(f"x_edge_loaded{n}") for n in range(RING)]
        aggr_gathered = [sem(f"aggr_gathered{n}") for n in range(2)]
        x_transposed, x_high, x_split = sem("x_transposed"), sem("x_high"), sem("x_split")
        aggr_transposed, aggr_high, aggr_split = (
            sem("aggr_transposed"), sem("aggr_high"), sem("aggr_split"))
        z1_done, h1_relu, h1_high, h1_split = (
            sem("z1_done"), sem("h1_relu"), sem("h1_high"), sem("h1_split"))
        z2_done, h2_relu, h2_high, h2_split = (
            sem("z2_done"), sem("h2_relu"), sem("h2_high"), sem("h2_split"))
        z3_done, xb3_done, y_summed = sem("z3_done"), sem("xb3_done"), sem("y_summed")
        stats_done, mean_var_done = sem("stats_done"), sem("mean_var_done")
        std_done, rstd_done, y_done = sem("std_done"), sem("rstd_done"), sem("y_done")
        bias_done, y_part_done = sem("bias_done"), sem("y_part_done")
        stored = [sem(f"stored{n}") for n in range(2)]
        scattered = [sem(f"scattered{n}") for n in range(RING)]
        dst_row_loaded = [sem(f"dst_row_loaded{n}") for n in range(RING)]
        dst_add_loaded = [sem(f"dst_add_loaded{n}") for n in range(2)]
        e_loaded = [sem(f"e_loaded{n}") for n in range(2)]
        n_before_done, to_spare_done, shift_done, own_known = (
            sem("n_before_done"), sem("to_spare_done"), sem("shift_done"), sem("own_known"))
        n_above_done, out_spare_done, out_shift_done, out_known = (
            sem("n_above_done"), sem("out_spare_done"), sem("out_shift_done"), sem("out_known"))
        cleared = sem("cleared")
        added = sem("added")
        pool_passed, dve_passed = sem("pool_passed"), sem("dve_passed")
        add_at_set, x_from_set, aggr_from_set, out_at_set = (
            sem("add_at_set"), sem("x_from_set"), sem("aggr_from_set"),
            sem("out_at_set"))
        dst_out_loaded = [sem(f"dst_out_loaded{n}") for n in range(2)]
        e_high, e_split = sem("e_high"), sem("e_split")
        same_done, sums_done, sums_copied = (
            sem("same_done"), sem("sums_done"), sem("sums_copied"))

        block = ctx.enter_context(nc.Block())

        def x_halves(step):
            return (a_hi, a_lo) if step.c == 1 else (x_hi, x_lo)

        def add_bias3(engine, vector, step):
            P, J = lanes(step.c), subs(step.c)
            if is_edge_step(step):
                f = step - FIRST_EDGE
                if f.c == 0:
                    engine.wait_ge(xb3_done, FIRST_EDGE)
                reached(engine, x_edge_loaded[step.slot(RING)], f.turns(RING, 16, 16))
            elif step.c == 0:
                engine.wait_ge(x_loaded_first, 16)
            else:
                reached(engine, x_loaded[step.c // 2 % 2], step.turns(4, 16, 16))
            reached(engine, y_summed, step.count(plus=-RING + 1))
            vector.tensor_tensor(
                xb3[0:P, step.slot(RING), 0:J, :], xin[0:P, step.c // 2 % 2, step.c % 2, 0:J, :],
                bias3[0:P, :].unsqueeze(1).to_broadcast([P, J, D]), ALU.add
            ).then_inc(xb3_done, 1)

        def pair_of(s):
            pair = s - ADD0
            if not 0 <= pair.c < PAIRS:
                return None
            group = pair.turns(2)
            if pair.c == PAIRS - 1:
                return pair, group, edge_lanes, 0, TAIL_SUB
            return pair, group, LANES, 2 * pair.slot(2), SUB

        def marking_group(s):
            if s.c > GROUPS:
                return None
            return (s, edge_lanes, TAIL_SUB) if s.c == GROUPS else (s, LANES, SUB)

        def dst_rows_of(rows, sub, n_lanes, n_sub):
            v = rows[0:n_lanes, 0:n_lanes * n_sub]
            return v.rearrange("q (p j) -> q j p", j=n_sub)[:, sub]

        @block.sync
        def _(sp):
            def load_tile(step):
                n = step.turns(2)
                if is_tail(step):
                    rows = x[PLAIN * STEP:nodes, :].rearrange("(p j) d -> p (j d)", j=2 * SUB)
                    to = xin[0:tail_lanes, step.c // 2 % 2, :, :, :]
                else:
                    rows = x[bass.ds(n * (2 * STEP), 2 * STEP), :].rearrange(
                        "(p j) d -> p (j d)", j=2 * SUB)
                    to = xin[:, step.c // 2 % 2, :, :, :]
                sp.dma_start(to.rearrange("p t j d -> p (t j d)"), rows).then_inc(
                    x_loaded[step.c // 2 % 2], 16)

            def load_dst_row(to, semaphore, group, n_edges_of):
                sp.dma_start(to[:, 0:n_edges_of],
                             dst[bass.ds(group * STEP, n_edges_of)].unsqueeze(0).to_broadcast(
                                 [LANES, n_edges_of])).then_inc(semaphore, 16)

            def load_edges(group_c, group, n_lanes, n_sub):
                sp.dma_start(e_in[0:n_lanes, group_c % 2, 0:n_sub, :].rearrange("p j d -> p (j d)"),
                             edges[bass.ds(group * STEP, n_lanes * n_sub), :].rearrange(
                                 "(p j) d -> p (j d)", j=n_sub)).then_inc(e_loaded[group_c % 2], 16)

            def load_weight(name, w):
                sp.dma_start(raw[name][:, :, :], w.rearrange("(k p) n -> p k n", p=LANES)).then_inc(
                    weights_loaded[name], 16)

            first = x[0:2 * STEP, :].rearrange("(p t j) d -> p t (j d)", t=2, j=SUB)
            sp.dma_start(xin[:, 0, 0, :, :].rearrange("p j d -> p (j d)"), first[:, 0]
                         ).then_inc(x_loaded_first, 16)
            load_weight("w1x", w1[0:D, :])
            sp.dma_start(xin[:, 0, 1, :, :].rearrange("p j d -> p (j d)"), first[:, 1]
                         ).then_inc(x_loaded[0], 16)
            load_weight("w2", w2)
            load_weight("w3", w3)
            load_weight("w1a", w1[D:2 * D, :])
            with nc.allow_non_contiguous_dma(reason="two biases of 256 words, once"):
                for to, b in ((bias1, b1), (bias2, b2)):
                    sp.dma_start(to[:, :], b.rearrange("(k p) -> p k", p=LANES)).then_inc(
                        biases_loaded, 16)
            sp.dma_start(bias3[:, :], b3.unsqueeze(0).to_broadcast([LANES, D])).then_inc(
                biases_loaded, 16)
            sp.dma_start(dst_i[:, 0:GROUPS * SUB].rearrange("p (g j) -> p g j", j=SUB),
                         dst[0:GROUPS * STEP].rearrange("(g p j) -> p g j", p=LANES, j=SUB)
                         ).then_inc(dst_loaded, 16)
            sp.dma_start(dst_i[0:edge_lanes, GROUPS * SUB:CHUNKS],
                         dst[GROUPS * STEP:n_edges].rearrange("(p j) -> p j", j=TAIL_SUB)
                         ).then_inc(dst_loaded, 16)
            for g in range(2):
                load_dst_row(dst_row[:, g, :], dst_row_loaded[g], g, STEP)
            load_tile(Step(0, 2))

            sp.wait_ge(constants, 5)

            def slot(s):
                if s.c < CLEARS:
                    sp.dma_start(table[bass.ds(s.count(CLEAR), CLEAR), :].rearrange(
                        "(p n j) d -> p n (j d)", p=LANES, j=ZERO_SUB),
                        zeros[:, :].unsqueeze(1).to_broadcast([LANES, CLEAR_RUNS, ZERO_SUB * D])
                    ).then_inc(cleared, 16)
                kept = s - 2 - ADD0
                if 0 <= kept.c < PAIRS and (kept.c % 2 == 1 or kept.c == PAIRS - 1):
                    half = kept.c // 2 % 2
                    P, J = (edge_lanes, TAIL_SUB) if kept.c == PAIRS - 1 else (LANES, SUB)
                    reached(sp, x_fetched[half], kept.turns(4, 16 * SUB, 16 * J))
                    sp.dma_start(x_edge[bass.ds(kept.turns(2) * STEP, P * J), :].rearrange(
                        "(p j) d -> p (j d)", j=J),
                        xg[0:P, half, 0:J, :].rearrange("p j d -> p (j d)")
                    ).then_inc(x_kept[half], 16)
                g = s + 2
                if g.c <= GROUPS:
                    reached(sp, own_known, g.count(plus=-3))
                    load_dst_row(dst_row[:, g.slot(RING), :], dst_row_loaded[g.slot(RING)],
                                 g.count(), edge_tail if g.c == GROUPS else STEP)
                ahead = s + 2 - ADD0
                if ahead.c >= 0 and ahead.c % 2 == 0 and ahead.c < PAIRS:
                    gc, group = ahead.c // 2, ahead.turns(2)
                    last = gc == GROUPS
                    reached(sp, sums_done, ahead.count(plus=-2))
                    load_dst_row(dst_add[:, gc % 2, :], dst_add_loaded[gc % 2], group,
                                 edge_tail if last else STEP)
                    load_edges(gc, group, edge_lanes if last else LANES, TAIL_SUB if last else SUB)
                if is_edge_step(s + 2):
                    f = s + 2 - FIRST_EDGE
                    if f.c == 0:
                        sp.wait_ge(same_done, PAIRS)
                    reached(sp, out_known, f.count(plus=-1))
                    load_dst_row(dst_add[:, f.slot(2), :], dst_out_loaded[f.slot(2)],
                                 f.count(), edge_tail if f.c == GROUPS else STEP)
                if s.c % 2 == 1 and s.c + 3 <= PLAIN:
                    reached(sp, x_transposed, s.count(plus=1))
                    reached(sp, xb3_done, s.count(plus=1))
                    load_tile(s + 3)
                if is_edge_step(s + 3):
                    step, f = s + 3, s + 3 - FIRST_EDGE
                    P, J = lanes(step.c), subs(step.c)
                    if f.c == 0:
                        for n in range(2):
                            sp.wait_ge(x_kept[n], 16 * ((GROUPS + 2 - n) // 2))
                    reached(sp, x_transposed, step.count(plus=-3))
                    reached(sp, xb3_done, step.count(plus=-3))
                    sp.dma_start(xin[0:P, step.c // 2 % 2, step.c % 2, 0:J, :].rearrange(
                        "p j d -> p (j d)"),
                        x_edge[bass.ds(f.count(STEP), P * J), :].rearrange(
                            "(p j) d -> p (j d)", j=J)
                    ).then_inc(x_edge_loaded[step.slot(RING)], 16)
                done = s - 4
                if done.c >= 0 and done.c % 2 == 0 and done.c <= PLAIN:
                    reached(sp, y_done, done.count(plus=2))
                    reached(sp, y_part_done, done.count(plus=2))
                    if is_tail(done):
                        rows = out[PLAIN * STEP:nodes, :].rearrange("(p j) d -> p (j d)", j=2 * SUB)
                        of = y[0:tail_lanes, done.c // 2 % 2, :, :, :]
                    else:
                        rows = out[bass.ds(done.turns(2) * (2 * STEP), 2 * STEP), :].rearrange(
                            "(p j) d -> p (j d)", j=2 * SUB)
                        of = y[:, done.c // 2 % 2, :, :, :]
                    sp.dma_start(rows, of.rearrange("p t j d -> p (t j d)")).then_inc(
                        stored[done.c // 2 % 2], 16)

            run_slots(sp, slot)
            for n in range(2):
                sp.wait_ge(stored[n], 16 * ((tiles + 2 - n) // 2))

        @block.gpsimd
        def _(pool):
            nc.gpsimd.memset(zeros[:, :], 0.0).then_inc(constants, 1)
            nc.gpsimd.memset(eps[:, :], EPS).then_inc(constants, 1)
            nc.gpsimd.iota(lane_i[:, :], pattern=[[0, 1]], base=nodes, channel_multiplier=1
                           ).then_inc(constants, 1)
            nc.gpsimd.memset(identity[:, :], 0.0).then_inc(masks_cleared, 1)
            nc.gpsimd.memset(earlier[:, :], 0.0).then_inc(masks_cleared, 1)
            pool.wait_ge(masks_cleared, 2)
            nc.gpsimd.affine_select(out=identity[:, :], in_=identity[:, :], compare_op=ALU.not_equal,
                                    fill=1.0, base=0, pattern=[[-1, LANES]], channel_multiplier=1
                                    ).then_inc(constants, 1)
            nc.gpsimd.affine_select(out=earlier[:, :], in_=earlier[:, :], compare_op=ALU.is_ge,
                                    fill=1.0, base=0, pattern=[[1, LANES]], channel_multiplier=-1
                                    ).then_inc(constants, 1)
            pool.wait_ge(biases_loaded, 48)
            pool.wait_ge(dst_loaded, 32)

            def apart():
                pool.sem_inc(pool_passed, 1)

            def list_rows(to, semaphore, of, group, half, P, J):
                apart()
                nc.gpsimd.tensor_copy(to[0:P, half, 0:J],
                                      of[0:P, bass.ds(group * SUB, J)]).then_inc(semaphore, 1)
                reached(pool, semaphore, group + 1)
                apart()

            add_bias3(pool, nc.gpsimd, Step(0, 0))

            def slot(s):
                if exists(s + 1) and not is_edge_step(s + 1):
                    add_bias3(pool, nc.gpsimd, s + 1)
                if now := pair_of(s):
                    pair, group, P, j0, J = now
                    if pair.c == 0:
                        pool.wait_ge(cleared, 16 * CLEARS)
                    half = pair.c // 2 % 2
                    reached(pool, added, pair.count(32))
                    if j0 == 0:
                        list_rows(add_at, add_at_set, own_i, group, half, P, J)
                        reached(pool, x_kept[half], pair.turns(4, 16))
                        list_rows(x_from, x_from_set, dst_i, group, half, P, J)

                    def fetch(j):
                        nc.gpsimd.indirect_dma_start(
                            out=xg[0:P, half, j, :], out_offset=None, in_=x[:, :],
                            in_offset=bass.IndirectOffsetOnAxis(ap=x_from[0:P, half, j:j + 1],
                                                                axis=0)
                        ).then_inc(x_fetched[half], 16)

                    apart()
                    fetch(j0)
                    reached(pool, sums_copied, pair.count(plus=1))
                    for j in range(2):
                        if j == 1:
                            fetch(j0 + 1)
                        reached(pool, added, pair.count(32, 16 * j))
                        apart()
                        nc.gpsimd.indirect_dma_start(
                            out=table[:, :], in_=sums[0:P, pair.slot(2), j, :], in_offset=None,
                            out_offset=bass.IndirectOffsetOnAxis(
                                ap=add_at[0:P, half, j0 + j:j0 + j + 1], axis=0),
                            compute_op=ALU.add).then_inc(added, 16)
                if is_edge_step(s + 2):
                    f = s + 2 - FIRST_EDGE
                    P, J = lanes(s.c + 2), subs(s.c + 2)
                    if f.c == 0:
                        pool.wait_ge(added, 16 * CHUNKS)
                    reached(pool, aggr_transposed, f.count(plus=-1))
                    list_rows(aggr_from, aggr_from_set, dst_i, f.count(), f.slot(2), P, J)
                    for j in range(J):
                        nc.gpsimd.indirect_dma_start(
                            out=aggr[0:P, f.slot(2), j, :], out_offset=None,
                            in_=table[:, :], in_offset=bass.IndirectOffsetOnAxis(
                                ap=aggr_from[0:P, f.slot(2), j:j + 1], axis=0)
                        ).then_inc(aggr_gathered[f.slot(2)], 16)
                if is_edge_step(s - 3):
                    step, f = s - 3, s - 3 - FIRST_EDGE
                    P, J = lanes(step.c), subs(step.c)
                    if f.c == 0:
                        for n in range(2):
                            pool.wait_ge(stored[n], 16 * ((tiles + 2 - n) // 2))
                    reached(pool, out_known, f.count(plus=1))
                    list_rows(out_at, out_at_set, out_i, f.count(), f.slot(2), P, J)
                    if J > act_norms(step):
                        reached(pool, y_done, step.count(plus=1))
                    reached(pool, y_part_done, step.count(plus=1))
                    if f.c >= 1:
                        reached(pool, scattered[(step - 1).slot(RING)],
                                (f - 1).turns(RING, 16 * SUB, 16 * SUB))
                    apart()
                    for j in range(J):
                        nc.gpsimd.indirect_dma_start(
                            out=out[:, :], in_=y[0:P, step.c // 2 % 2, step.c % 2, j, :],
                            in_offset=None, out_offset=bass.IndirectOffsetOnAxis(
                                ap=out_at[0:P, f.slot(2), j:j + 1], axis=0),
                            bounds_check=nodes - 1, oob_is_err=False
                        ).then_inc(scattered[step.slot(RING)], 16)

            run_slots(pool, slot)
            for n in range(RING):
                uses = [c for c in range(FIRST_EDGE, STEPS) if c % RING == n]
                pool.wait_ge(scattered[n], 16 * sum(subs(c) for c in uses))

        @block.scalar
        def _(act):
            def high_of_weight(name):
                act.wait_ge(weights_loaded[name], 16)
                nc.scalar.copy(w_hi[name][:, :, :], raw[name][:, :, :]).then_inc(weights_high, 1)

            def high_of_x(step):
                N = lanes(step.c) * subs(step.c)
                reached(act, x_transposed, step.count(plus=1))
                nc.scalar.copy(x_halves(step)[0][:, :, 0:N], xT[:, :, 0:N]).then_inc(x_high, 1)

            def relu_of(step, z, bias, kept, hi, z_done, relu_done, high_done, split_done):
                N = lanes(step.c) * subs(step.c)
                reached(act, split_done, step.count())
                for m in range(KD):
                    reached(act, z_done, step.count(KD, m + 1))
                    nc.scalar.activation(kept[:, m, 0:N], z[:, m, 0:N], ACT.Relu,
                                         bias=bias[:, m:m + 1]).then_inc(relu_done, 1)
                    nc.scalar.activation(hi[:, step.slot(2), m, 0:N], z[:, m, 0:N], ACT.Relu,
                                         bias=bias[:, m:m + 1]).then_inc(high_done, 1)

            high_of_weight("w1x")
            high_of_x(Step(0, 0))
            for name in ("w2", "w3", "w1a"):
                high_of_weight(name)
            act.wait_ge(biases_loaded, 48)
            act.wait_ge(constants, 5)
            high_of_x(Step(0, 1))

            def slot(s):
                if exists(s):
                    relu_of(s, z1, bias1, h[:, 0], h1_hi, z1_done, h1_relu, h1_high, h1_split)
                if exists(s + 1) and s.c > 0:
                    high_of_x(s + 1)
                if now := pair_of(s + 1):
                    pair, _, P, j0, _ = now
                    reached(act, e_loaded[pair.c // 2 % 2], pair.turns(4, 16, 16))
                    reached(act, sums_done, pair.count(plus=-1))
                    nc.scalar.copy(e_hi[0:P, pair.slot(2), :, :],
                                   e_in[0:P, pair.c // 2 % 2, j0:j0 + 2, :]).then_inc(e_high, 1)
                if exists(s - 3):
                    step = s - 3
                    P, J = lanes(step.c), subs(step.c)
                    reached(act, mean_var_done, step.count(SUB, J))
                    nc.scalar.activation(std[0:P, step.slot(2), 0:J],
                                         mean_var[0:P, step.slot(2), 0:J, 1], ACT.Sqrt,
                                         bias=eps[0:P, :]).then_inc(std_done, 1)
                if exists(s - 1):
                    relu_of(s - 1, z2, bias2, h[:, 1], h2_hi, z2_done, h2_relu, h2_high, h2_split)
                if now := pair_of(s):
                    pair, _, P, _, _ = now
                    reached(act, sums_done, pair.count(plus=1))
                    reached(act, added, pair.count(32, -32))
                    nc.scalar.copy(sums[0:P, pair.slot(2), :, :],
                                   xT[0:P, 0, :].rearrange("p (j d) -> p j d", j=2)
                                   ).then_inc(sums_copied, 1)
                if is_edge_step(s + 1):
                    f = s + 1 - FIRST_EDGE
                    N = lanes(s.c + 1) * subs(s.c + 1)
                    reached(act, aggr_transposed, f.count(plus=1))
                    nc.scalar.copy(a_hi[:, :, 0:N], xT[:, :, 0:N]).then_inc(aggr_high, 1)

                if exists(s - 3):
                    step = s - 3
                    P, J = lanes(step.c), subs(step.c)
                    reached(act, bias_done, step.count(plus=1))
                    for j in range(J - act_norms(step), J):
                        rows = y[0:P, step.c // 2 % 2, step.c % 2, j, :]
                        last = nc.scalar.activation(rows, rows, ACT.Identity,
                                                    bias=minus_mean[0:P, j:j + 1],
                                                    scale=rstd[0:P, j:j + 1])
                    last.then_inc(y_part_done, 1)

            run_slots(act, slot)

        @block.vector
        def _(dve):
            def low_of_weight(n, name):
                dve.wait_ge(weights_high, n + 1)
                nc.vector.tensor_tensor(w_lo[name][:, :, :], raw[name][:, :, :],
                                        w_hi[name][:, :, :].bitcast(FP32), ALU.subtract
                                        ).then_inc(weights_split, 1)

            def low_of_x(step):
                N = lanes(step.c) * subs(step.c)
                reached(dve, x_high, step.count(plus=1))
                hi, lo = x_halves(step)
                nc.vector.tensor_tensor(lo[:, :, 0:N], xT[:, :, 0:N],
                                        hi[:, :, 0:N].bitcast(FP32), ALU.subtract
                                        ).then_inc(x_split, 1)

            def low_of_h(step, kept, hi, lo, relu_done, high_done, split_done):
                N = lanes(step.c) * subs(step.c)
                reached(dve, relu_done, step.count(KD, KD))
                reached(dve, high_done, step.count(KD, KD))
                nc.vector.tensor_tensor(lo[:, step.slot(2), :, 0:N], kept[:, :, 0:N],
                                        hi[:, step.slot(2), :, 0:N].bitcast(FP32), ALU.subtract
                                        ).then_inc(split_done, 1)

            def to_spare_rows(which, of, cols, P, J, done):
                nc.vector.tensor_scalar(to_spare[0:P, which, 0:J], of[0:P, cols], -1.0,
                                        lane[0:P, :], ALU.mult, ALU.add).then_inc(done, 1)

            def shift_rows(which, n, P, J, done):
                nc.vector.scalar_tensor_tensor(
                    out=shift[0:P, which, 0:J], in0=n[0:P, 0:J], scalar=1.0,
                    in1=to_spare[0:P, which, 0:J], op0=ALU.min, op1=ALU.mult).then_inc(done, 1)

            def mark_count(group, P, J):
                reached(dve, dst_row_loaded[group.slot(RING)], group.turns(RING, 16, 16))
                reached(dve, own_known, group.count())
                to_spare_rows(0, dst_f, bass.ds(group.count(SUB), J), P, J, to_spare_done)
                for j in range(J):
                    nc.vector.scalar_tensor_tensor(
                        out=before[0:P, j, 0:P],
                        in0=dst_rows_of(dst_row[:, group.slot(RING), :], j, P, J),
                        scalar=dst_f[0:P, bass.ds(group.count(SUB, j), 1)], in1=earlier[0:P, 0:P],
                        op0=ALU.is_equal, op1=ALU.mult, accum_out=n_before[0:P, j:j + 1]
                    ).then_inc(n_before_done, 1)

            def mark_shift(group, P, J):
                reached(dve, n_before_done, group.count(SUB, J))
                reached(dve, to_spare_done, group.count(plus=1))
                shift_rows(0, n_before, P, J, shift_done)

            def mark_own(group, P, J):
                cols = bass.ds(group.count(SUB), J)
                reached(dve, shift_done, group.count(plus=1))
                nc.vector.tensor_tensor(own_i[0:P, cols], shift[0:P, 0, 0:J], dst_f[0:P, cols],
                                        ALU.add).then_inc(own_known, 1)

            def mark_out_count(group, P, J):
                reached(dve, dst_out_loaded[group.slot(2)], group.turns(2, 16, 16))
                reached(dve, out_known, group.count())
                to_spare_rows(1, own_i, bass.ds(group.count(SUB), J), P, J, out_spare_done)
                for j in range(1, J):
                    nc.vector.tensor_scalar(
                        above[0:P, j * (j - 1) // 2:j * (j + 1) // 2, 0:P],
                        dst_rows_of(dst_add[:, group.slot(2), :], slice(0, j), P, J),
                        dst_f[0:P, bass.ds(group.count(SUB, j), 1)], None, ALU.is_equal, ALU.add,
                        accum_out=n_above[0:P, j:j + 1]).then_inc(n_above_done, 1)

            def mark_out_shift(group, P, J):
                reached(dve, n_above_done, group.count(SUB - 1, J - 1))
                reached(dve, out_spare_done, group.count(plus=1))
                shift_rows(1, n_above, P, J, out_shift_done)

            def mark_out_row(group, P, J):
                cols = bass.ds(group.count(SUB), J)
                reached(dve, out_shift_done, group.count(plus=1))
                nc.vector.tensor_tensor(out_i[0:P, cols], shift[0:P, 1, 0:J], own_i[0:P, cols],
                                        ALU.add).then_inc(out_known, 1)

            low_of_weight(0, "w1x")
            low_of_x(Step(0, 0))
            for n, name in enumerate(("w2", "w3", "w1a")):
                low_of_weight(n + 1, name)
            dve.wait_ge(constants, 5)
            dve.wait_ge(dst_loaded, 32)
            nc.vector.tensor_copy(lane[:, :], lane_i[:, :]).then_inc(spare_known, 1)
            nc.vector.tensor_copy(dst_f[:, 0:GROUPS * SUB], dst_i[:, 0:GROUPS * SUB]
                                  ).then_inc(dst_f_known, 1)
            nc.vector.tensor_copy(dst_f[0:edge_lanes, GROUPS * SUB:CHUNKS],
                                  dst_i[0:edge_lanes, GROUPS * SUB:CHUNKS]).then_inc(dst_f_known, 1)
            nc.vector.memset(n_above[:, :], 0.0).then_inc(spare_known, 1)
            dve.wait_ge(spare_known, 2)
            dve.wait_ge(dst_f_known, 2)

            def slot(s):
                if exists(s + 1):
                    low_of_x(s + 1)
                if exists(s):
                    low_of_h(s, h[:, 0], h1_hi, h1_lo, h1_relu, h1_high, h1_split)
                marked, now, marks_out = marking_group(s), pair_of(s), is_edge_step(s)
                step = s - 3
                P4, J4 = lanes(step.c), subs(step.c)
                if exists(step):
                    reached(dve, std_done, step.count(plus=1))
                    reached(dve, y_done, step.count())
                    reached(dve, y_part_done, step.count())
                    nc.vector.reciprocal(rstd[0:P4, 0:J4], std[0:P4, step.slot(2), 0:J4]
                                         ).then_inc(rstd_done, 1)
                if now:
                    pair, group, P, j0, J = now
                    gc = pair.c // 2
                    reached(dve, dst_add_loaded[gc % 2], pair.turns(4, 16, 16))
                    reached(dve, sums_done, pair.count(plus=-1))
                    for j in range(2):
                        last = nc.vector.tensor_scalar(
                            same[0:P, pair.slot(2), j, 0:P],
                            dst_rows_of(dst_add[:, gc % 2, :], j0 + j, P, J),
                            dst_f[0:P, bass.ds(group * SUB + j0 + j, 1)], None, ALU.is_equal)
                    last.then_inc(same_done, 1)
                if exists(step):
                    reached(dve, rstd_done, step.count(plus=1))
                    nc.vector.scalar_tensor_tensor(
                        out=minus_mean[0:P4, 0:J4], in0=mean_var[0:P4, step.slot(2), 0:J4, 0],
                        scalar=-1.0, in1=rstd[0:P4, 0:J4], op0=ALU.mult, op1=ALU.mult
                    ).then_inc(bias_done, 1)
                if after := pair_of(s + 1):
                    pair, _, P, j0, _ = after
                    reached(dve, e_high, pair.count(plus=1))
                    nc.vector.tensor_tensor(e_lo[0:P, pair.slot(2), :, :],
                                            e_in[0:P, pair.c // 2 % 2, j0:j0 + 2, :],
                                            e_hi[0:P, pair.slot(2), :, :].bitcast(FP32),
                                            ALU.subtract).then_inc(e_split, 1)
                if marked:
                    mark_count(*marked)
                if exists(step):
                    for j in range(J4 - act_norms(step)):
                        rows = y[0:P4, step.c // 2 % 2, step.c % 2, j, :]
                        last = nc.vector.tensor_scalar(
                            rows, rows, mean_var[0:P4, step.slot(2), j, 0:1], rstd[0:P4, j:j + 1],
                            ALU.subtract, ALU.mult)
                    if J4 > act_norms(step):
                        last.then_inc(y_done, 1)
                if marked:
                    mark_shift(*marked)
                if is_edge_step(s + 1):
                    f = s + 1 - FIRST_EDGE
                    N = lanes(s.c + 1) * subs(s.c + 1)
                    reached(dve, aggr_high, f.count(plus=1))
                    nc.vector.tensor_tensor(a_lo[:, :, 0:N], xT[:, :, 0:N],
                                            a_hi[:, :, 0:N].bitcast(FP32), ALU.subtract
                                            ).then_inc(aggr_split, 1)
                if exists(s - 1):
                    low_of_h(s - 1, h[:, 1], h2_hi, h2_lo, h2_relu, h2_high, h2_split)
                if marked:
                    mark_own(*marked)
                if exists(s - 2):
                    step = s - 2
                    P, J = lanes(step.c), subs(step.c)
                    reached(dve, z3_done, step.count(plus=1))
                    reached(dve, xb3_done, step.count(plus=1))
                    if step.c - RING >= FIRST_EDGE:
                        reached(dve, scattered[step.slot(RING)],
                                (step - FIRST_EDGE).turns(RING, 16 * SUB))
                    else:
                        reached(dve, stored[step.c // 2 % 2], step.turns(4, 16))
                    rows = y[0:P, step.c // 2 % 2, step.c % 2, 0:J, :]
                    nc.vector.tensor_tensor(rows, z3[0:P, 0:J, :], xb3[0:P, step.slot(RING), 0:J, :],
                                            ALU.add).then_inc(y_summed, 1)
                    reached(dve, y_summed, step.count(plus=1))
                    reached(dve, mean_var_done, step.count(SUB))
                    for j in range(J):
                        nc.vector.bn_stats(stats[0:P, j, :], rows[:, j, :]).then_inc(stats_done, 1)
                if marks_out:
                    out_group = (s - FIRST_EDGE, lanes(s.c), subs(s.c))
                    mark_out_count(*out_group)
                if exists(s - 2):
                    P, J = lanes(s.c - 2), subs(s.c - 2)
                    for j in range(J):
                        reached(dve, stats_done, step.count(SUB, j + 1))
                        dve.sem_inc(dve_passed, 1)
                        nc.vector.bn_aggr(mean_var[0:P, step.slot(2), j, :], stats[0:P, j, :]
                                          ).then_inc(mean_var_done, 1)
                if marks_out:
                    mark_out_shift(*out_group)
                    mark_out_row(*out_group)
                if is_edge_step(s + 1):
                    add_bias3(dve, nc.vector, s + 1)

            run_slots(dve, slot)

        @block.tensor
        def _(pe):
            pe.wait_ge(constants, 5)

            def transpose(step, of, done):
                P, J = lanes(step.c), subs(step.c)
                for k in range(KD):
                    for j in range(J):
                        last = nc.tensor.transpose(xT[:, k, j * P:(j + 1) * P],
                                                   of[0:P, j, k * LANES:(k + 1) * LANES],
                                                   identity[0:P, 0:P])
                last.then_inc(done, 1)

            def transpose_x(step):
                if is_edge_step(step):
                    f = step - FIRST_EDGE
                    reached(pe, x_edge_loaded[step.slot(RING)], f.turns(RING, 16, 16))
                    reached(pe, aggr_split, f.count())
                elif step.c == 0:
                    pe.wait_ge(x_loaded_first, 16)
                else:
                    reached(pe, x_loaded[step.c // 2 % 2], step.turns(4, 16, 16))
                    reached(pe, x_split, step.count())
                    if now := pair_of(step - 2):
                        reached(pe, sums_copied, now[0].count(plus=1))
                transpose(step, xin[:, step.c // 2 % 2, step.c % 2, :, :], x_transposed)

            def layer(step, z, operands, z_used, done):
                N = lanes(step.c) * subs(step.c)
                for m in range(KD):
                    reached(pe, z_used, step.count(KD, m + 1 - KD))
                    passes = [(w[:, k, m * LANES:(m + 1) * LANES], v[:, k, 0:N])
                              for name, v_hi, v_lo in operands
                              for w, v in ((w_hi[name], v_hi), (w_lo[name], v_hi),
                                           (w_hi[name], v_lo))
                              for k in range(KD)]
                    for n, (w, v) in enumerate(passes):
                        if m == 0 and n == 3 * KD:
                            reached(pe, aggr_split, (step - FIRST_EDGE).count(plus=1))
                        last = nc.tensor.matmul(z[:, m, 0:N], w, v, start=n == 0,
                                                stop=n == len(passes) - 1)
                    last.then_inc(done, 1)

            def transpose_aggr(step):
                f = step - FIRST_EDGE
                reached(pe, aggr_gathered[f.slot(2)], f.turns(2, 16 * SUB, 16 * subs(step.c)))
                reached(pe, x_split, step.count(plus=1))
                transpose(step, aggr[:, f.slot(2), :, :], aggr_transposed)

            transpose_x(Step(0, 0))
            transpose_x(Step(0, 1))

            def slot(s):
                if s.c < len(raw):
                    pe.wait_ge(weights_split, s.c + 1)
                if exists(s):
                    reached(pe, x_split, s.count(plus=1))
                    operands = [("w1x", *x_halves(s))]
                    if is_edge_step(s):
                        operands.append(("w1a", a_hi, a_lo))
                    layer(s, z1, operands, h1_high, z1_done)
                if exists(s + 1) and s.c > 0:
                    transpose_x(s + 1)
                if exists(s - 1):
                    step = s - 1
                    reached(pe, h1_split, step.count(plus=1))
                    layer(step, z2, [("w2", h1_hi[:, step.slot(2)], h1_lo[:, step.slot(2)])],
                          h2_high, z2_done)
                if exists(s - 2):
                    step = s - 2
                    P, J = lanes(step.c), subs(step.c)
                    reached(pe, h2_split, step.count(plus=1))
                    reached(pe, y_summed, step.count())
                    hi, lo = h2_hi[:, step.slot(2)], h2_lo[:, step.slot(2)]
                    for j in range(J):
                        cols = slice(j * P, (j + 1) * P)
                        passes = [(v[:, k, cols], w["w3"][:, k, :])
                                  for v, w in ((hi, w_hi), (hi, w_lo), (lo, w_hi))
                                  for k in range(KD)]
                        for n, (v, w) in enumerate(passes):
                            last = nc.tensor.matmul(z3[0:P, j, :], v, w, start=n == 0,
                                                    stop=n == len(passes) - 1)
                        if j == 0 and is_edge_step(s + 1):
                            transpose_aggr(s + 1)
                    last.then_inc(z3_done, 1)
                if now := pair_of(s):
                    pair, _, P, j0, _ = now
                    reached(pe, same_done, pair.count(plus=1))
                    reached(pe, e_split, pair.count(plus=1))
                    reached(pe, x_split, s.count(plus=2))
                    for j in range(2):
                        for n, e in enumerate((e_hi, e_lo)):
                            last = nc.tensor.matmul(xT[0:P, 0, j * D:(j + 1) * D],
                                                    same[0:P, pair.slot(2), j, 0:P],
                                                    e[0:P, pair.slot(2), j, :],
                                                    start=n == 0, stop=n == 1)
                    last.then_inc(sums_done, 1)

            run_slots(pe, slot)


_INS = ['x', 'src', 'dst', 'edge_attr_256', 'L0_gnn_W1', 'L0_gnn_b1', 'L0_gnn_W2', 'L0_gnn_b2',
        'L0_gnn_W3', 'L0_gnn_b3']


def kernel(**inputs):
    import numpy as _np
    import concourse.bacc as _bacc
    from concourse import mybir as _mybir
    from concourse.bass_utils import run_bass_kernel_spmd as _run

    nc = _bacc.Bacc("TRN2", target_bir_lowering=False, num_devices=1)
    arrays, args = {}, []
    for name in _INS:
        a = _np.ascontiguousarray(inputs[name])
        arrays[f"in_{name}_dram"] = a
        args.append(nc.dram_tensor(f"in_{name}_dram", a.shape, _mybir.dt.from_np(a.dtype),
                                   kind="ExternalInput").ap())
    out = nc.dram_tensor("out_0_dram", args[0].shape, _mybir.dt.float32, kind="ExternalOutput").ap()
    bass_gnn_residual_norm(nc, *args, out)
    r = _run(nc, [arrays], core_ids=[0])
    return r.results[0]["out_0_dram"]
```
